# Optimizing a Trainium2 kernel written in Bass

```python
import numpy as np
import jax
import jax.numpy as jnp

def _softmax(x, axis=-1):
    return jax.nn.softmax(x, axis=axis)

def _gelu(x):
    return jax.nn.gelu(x, approximate=True)

def _silu(x):
    return jax.nn.silu(x)

def _sigmoid(x):
    return jax.nn.sigmoid(x)

def _layernorm(x, axis=-1, eps=1e-05):
    m = jnp.mean(x, axis=axis, keepdims=True)
    v = jnp.var(x, axis=axis, keepdims=True)
    return (x - m) / jnp.sqrt(v + eps)

def _scatter_add(tgt, idx, src, axis=0):
    return tgt.at[idx].add(src)

def _segment_sum(src, seg, n):
    return jax.ops.segment_sum(src, seg, n)
kernel_name = 'mk_dlrm_tower_d1_rec_r8_3f5d0b'

def setup_inputs(seed: int=0):
    np.random.seed(seed)
    _w = jnp.asarray

    def _rec_inputs():
        import jax
        import jax.numpy as jnp
        _tk = jax.random.key(seed)
        dense_ctx = jax.random.normal(jax.random.fold_in(_tk, 190), (1024, 16), jnp.float32)
        ids = jnp.stack([jax.random.randint(jax.random.fold_in(_tk, 200 + f), (1024,), 0, v, jnp.int32) for f, v in enumerate([1000, 12500, 1000, 125000, 12500, 12500, 125000, 125000, 12500, 1000, 12500, 1250, 12500, 1000, 1000, 1000, 125000, 1000, 125000, 1000, 1000, 1250, 125000, 1000, 1000, 12500, 12500, 12500, 1000, 1250, 125000, 1000, 12500, 1000, 1000, 125000, 1000, 12500, 1250])], axis=1)
        tbl_0 = 0.05 * jax.random.normal(jax.random.fold_in(_tk, 500 + 0), (1000, 16), jnp.float32)
        tbl_1 = 0.05 * jax.random.normal(jax.random.fold_in(_tk, 500 + 1), (12500, 16), jnp.float32)
        tbl_2 = 0.05 * jax.random.normal(jax.random.fold_in(_tk, 500 + 2), (1000, 16), jnp.float32)
        tbl_3 = 0.05 * jax.random.normal(jax.random.fold_in(_tk, 500 + 3), (125000, 16), jnp.float32)
        tbl_4 = 0.05 * jax.random.normal(jax.random.fold_in(_tk, 500 + 4), (12500, 16), jnp.float32)
        tbl_5 = 0.05 * jax.random.normal(jax.random.fold_in(_tk, 500 + 5), (12500, 16), jnp.float32)
        tbl_6 = 0.05 * jax.random.normal(jax.random.fold_in(_tk, 500 + 6), (125000, 16), jnp.float32)
        tbl_7 = 0.05 * jax.random.normal(jax.random.fold_in(_tk, 500 + 7), (125000, 16), jnp.float32)
        tbl_8 = 0.05 * jax.random.normal(jax.random.fold_in(_tk, 500 + 8), (12500, 16), jnp.float32)
        tbl_9 = 0.05 * jax.random.normal(jax.random.fold_in(_tk, 500 + 9), (1000, 16), jnp.float32)
        tbl_10 = 0.05 * jax.random.normal(jax.random.fold_in(_tk, 500 + 10), (12500, 16), jnp.float32)
        tbl_11 = 0.05 * jax.random.normal(jax.random.fold_in(_tk, 500 + 11), (1250, 16), jnp.float32)
        tbl_12 = 0.05 * jax.random.normal(jax.random.fold_in(_tk, 500 + 12), (12500, 16), jnp.float32)
        tbl_13 = 0.05 * jax.random.normal(jax.random.fold_in(_tk, 500 + 13), (1000, 16), jnp.float32)
        tbl_14 = 0.05 * jax.random.normal(jax.random.fold_in(_tk, 500 + 14), (1000, 16), jnp.float32)
        tbl_15 = 0.05 * jax.random.normal(jax.random.fold_in(_tk, 500 + 15), (1000, 16), jnp.float32)
        tbl_16 = 0.05 * jax.random.normal(jax.random.fold_in(_tk, 500 + 16), (125000, 16), jnp.float32)
        tbl_17 = 0.05 * jax.random.normal(jax.random.fold_in(_tk, 500 + 17), (1000, 16), jnp.float32)
        tbl_18 = 0.05 * jax.random.normal(jax.random.fold_in(_tk, 500 + 18), (125000, 16), jnp.float32)
        tbl_19 = 0.05 * jax.random.normal(jax.random.fold_in(_tk, 500 + 19), (1000, 16), jnp.float32)
        tbl_20 = 0.05 * jax.random.normal(jax.random.fold_in(_tk, 500 + 20), (1000, 16), jnp.float32)
        tbl_21 = 0.05 * jax.random.normal(jax.random.fold_in(_tk, 500 + 21), (1250, 16), jnp.float32)
        tbl_22 = 0.05 * jax.random.normal(jax.random.fold_in(_tk, 500 + 22), (125000, 16), jnp.float32)
        tbl_23 = 0.05 * jax.random.normal(jax.random.fold_in(_tk, 500 + 23), (1000, 16), jnp.float32)
        tbl_24 = 0.05 * jax.random.normal(jax.random.fold_in(_tk, 500 + 24), (1000, 16), jnp.float32)
        tbl_25 = 0.05 * jax.random.normal(jax.random.fold_in(_tk, 500 + 25), (12500, 16), jnp.float32)
        tbl_26 = 0.05 * jax.random.normal(jax.random.fold_in(_tk, 500 + 26), (12500, 16), jnp.float32)
        tbl_27 = 0.05 * jax.random.normal(jax.random.fold_in(_tk, 500 + 27), (12500, 16), jnp.float32)
        tbl_28 = 0.05 * jax.random.normal(jax.random.fold_in(_tk, 500 + 28), (1000, 16), jnp.float32)
        tbl_29 = 0.05 * jax.random.normal(jax.random.fold_in(_tk, 500 + 29), (1250, 16), jnp.float32)
        tbl_30 = 0.05 * jax.random.normal(jax.random.fold_in(_tk, 500 + 30), (125000, 16), jnp.float32)
        tbl_31 = 0.05 * jax.random.normal(jax.random.fold_in(_tk, 500 + 31), (1000, 16), jnp.float32)
        tbl_32 = 0.05 * jax.random.normal(jax.random.fold_in(_tk, 500 + 32), (12500, 16), jnp.float32)
        tbl_33 = 0.05 * jax.random.normal(jax.random.fold_in(_tk, 500 + 33), (1000, 16), jnp.float32)
        tbl_34 = 0.05 * jax.random.normal(jax.random.fold_in(_tk, 500 + 34), (1000, 16), jnp.float32)
        tbl_35 = 0.05 * jax.random.normal(jax.random.fold_in(_tk, 500 + 35), (125000, 16), jnp.float32)
        tbl_36 = 0.05 * jax.random.normal(jax.random.fold_in(_tk, 500 + 36), (1000, 16), jnp.float32)
        tbl_37 = 0.05 * jax.random.normal(jax.random.fold_in(_tk, 500 + 37), (12500, 16), jnp.float32)
        tbl_38 = 0.05 * jax.random.normal(jax.random.fold_in(_tk, 500 + 38), (1250, 16), jnp.float32)
        _rk = jax.random.fold_in(_tk, 7)
        W_top1 = 0.05 * jax.random.normal(jax.random.fold_in(_tk, 801), (400, 512), jnp.float32)
        W_top2 = 0.0441942 * jax.random.normal(jax.random.fold_in(_tk, 802), (512, 256), jnp.float32)
        W_top3 = 0.0625 * jax.random.normal(jax.random.fold_in(_tk, 803), (256, 1), jnp.float32)
        b_top1 = jnp.zeros((512,), jnp.float32)
        b_top2 = jnp.zeros((256,), jnp.float32)
        return (dense_ctx, ids, tbl_0, tbl_1, tbl_2, tbl_3, tbl_4, tbl_5, tbl_6, tbl_7, tbl_8, tbl_9, tbl_10, tbl_11, tbl_12, tbl_13, tbl_14, tbl_15, tbl_16, tbl_17, tbl_18, tbl_19, tbl_20, tbl_21, tbl_22, tbl_23, tbl_24, tbl_25, tbl_26, tbl_27, tbl_28, tbl_29, tbl_30, tbl_31, tbl_32, tbl_33, tbl_34, tbl_35, tbl_36, tbl_37, tbl_38, W_top1, b_top1, W_top2, b_top2, W_top3)
    dense_ctx, ids, tbl_0, tbl_1, tbl_2, tbl_3, tbl_4, tbl_5, tbl_6, tbl_7, tbl_8, tbl_9, tbl_10, tbl_11, tbl_12, tbl_13, tbl_14, tbl_15, tbl_16, tbl_17, tbl_18, tbl_19, tbl_20, tbl_21, tbl_22, tbl_23, tbl_24, tbl_25, tbl_26, tbl_27, tbl_28, tbl_29, tbl_30, tbl_31, tbl_32, tbl_33, tbl_34, tbl_35, tbl_36, tbl_37, tbl_38, W_top1, b_top1, W_top2, b_top2, W_top3 = _rec_inputs()

    def _L0_rec_setup():
        import jax, jax.numpy as jnp
        import numpy as np
        M_FIELDS = 39
        EMB_D = 16
        UNITS = [128, 128, 128]
        BATCH = 256

        def _cin_forward(x, ws, bs):
            b, m, D = x.shape
            prev = x
            logit = []
            for k in range(len(ws)):
                h = prev.shape[1]
                z = jnp.einsum('bmd,bhd->bdmh', x, prev).reshape(b, D, m * h)
                t = jnp.einsum('bdc,co->bdo', z, ws[k]) + bs[k]
                t = jnp.transpose(t, (0, 2, 1))
                norm = jnp.sqrt(jnp.sum(t * t, axis=(-2, -1), keepdims=True))
                t = t / norm
                logit.append(t)
                prev = t
            return jnp.sum(jnp.concatenate(logit, axis=1), axis=-1)
        key = jax.random.key(seed)
        ks = jax.random.split(key, 4)
        x = jax.random.normal(ks[0], (BATCH, M_FIELDS, EMB_D), dtype=jnp.float32)
        w0 = jax.random.normal(ks[1], (M_FIELDS * M_FIELDS, UNITS[0]), dtype=jnp.float32) * 0.05
        w1 = jax.random.normal(ks[2], (UNITS[0] * M_FIELDS, UNITS[1]), dtype=jnp.float32) * 0.05
        w2 = jax.random.normal(ks[3], (UNITS[1] * M_FIELDS, UNITS[2]), dtype=jnp.float32) * 0.05
        b0 = jnp.zeros((UNITS[0],), dtype=jnp.float32)
        b1 = jnp.zeros((UNITS[1],), dtype=jnp.float32)
        b2 = jnp.zeros((UNITS[2],), dtype=jnp.float32)
        return {'x': x, 'w0': w0, 'w1': w1, 'w2': w2, 'b0': b0, 'b1': b1, 'b2': b2}
    _L0_rec_all = _L0_rec_setup()
    _L0_rec_in = {k: v for k, v in _L0_rec_all.items() if k in ('w0', 'w1', 'w2', 'b0', 'b1', 'b2')}
    del _L0_rec_all
    return {'dense_ctx': dense_ctx, 'ids': ids, 'tbl_0': tbl_0, 'tbl_1': tbl_1, 'tbl_2': tbl_2, 'tbl_3': tbl_3, 'tbl_4': tbl_4, 'tbl_5': tbl_5, 'tbl_6': tbl_6, 'tbl_7': tbl_7, 'tbl_8': tbl_8, 'tbl_9': tbl_9, 'tbl_10': tbl_10, 'tbl_11': tbl_11, 'tbl_12': tbl_12, 'tbl_13': tbl_13, 'tbl_14': tbl_14, 'tbl_15': tbl_15, 'tbl_16': tbl_16, 'tbl_17': tbl_17, 'tbl_18': tbl_18, 'tbl_19': tbl_19, 'tbl_20': tbl_20, 'tbl_21': tbl_21, 'tbl_22': tbl_22, 'tbl_23': tbl_23, 'tbl_24': tbl_24, 'tbl_25': tbl_25, 'tbl_26': tbl_26, 'tbl_27': tbl_27, 'tbl_28': tbl_28, 'tbl_29': tbl_29, 'tbl_30': tbl_30, 'tbl_31': tbl_31, 'tbl_32': tbl_32, 'tbl_33': tbl_33, 'tbl_34': tbl_34, 'tbl_35': tbl_35, 'tbl_36': tbl_36, 'tbl_37': tbl_37, 'tbl_38': tbl_38, 'W_top1': W_top1, 'b_top1': b_top1, 'W_top2': W_top2, 'b_top2': b_top2, 'W_top3': W_top3, 'L0_rec_w0': _L0_rec_in['w0'], 'L0_rec_w1': _L0_rec_in['w1'], 'L0_rec_w2': _L0_rec_in['w2'], 'L0_rec_b0': _L0_rec_in['b0'], 'L0_rec_b1': _L0_rec_in['b1'], 'L0_rec_b2': _L0_rec_in['b2']}

def reference(dense_ctx, ids, tbl_0, tbl_1, tbl_2, tbl_3, tbl_4, tbl_5, tbl_6, tbl_7, tbl_8, tbl_9, tbl_10, tbl_11, tbl_12, tbl_13, tbl_14, tbl_15, tbl_16, tbl_17, tbl_18, tbl_19, tbl_20, tbl_21, tbl_22, tbl_23, tbl_24, tbl_25, tbl_26, tbl_27, tbl_28, tbl_29, tbl_30, tbl_31, tbl_32, tbl_33, tbl_34, tbl_35, tbl_36, tbl_37, tbl_38, W_top1, b_top1, W_top2, b_top2, W_top3, L0_rec_w0, L0_rec_w1, L0_rec_w2, L0_rec_b0, L0_rec_b1, L0_rec_b2):
    import jax
    import jax.numpy as jnp

    def _L0_rec_ref(x, w0, w1, w2, b0, b1, b2):
        import jax, jax.numpy as jnp
        import numpy as np
        M_FIELDS = 39
        EMB_D = 16
        UNITS = [128, 128, 128]
        BATCH = 256

        def _cin_forward(x, ws, bs):
            b, m, D = x.shape
            prev = x
            logit = []
            for k in range(len(ws)):
                h = prev.shape[1]
                z = jnp.einsum('bmd,bhd->bdmh', x, prev).reshape(b, D, m * h)
                t = jnp.einsum('bdc,co->bdo', z, ws[k]) + bs[k]
                t = jnp.transpose(t, (0, 2, 1))
                norm = jnp.sqrt(jnp.sum(t * t, axis=(-2, -1), keepdims=True))
                t = t / norm
                logit.append(t)
                prev = t
            return jnp.sum(jnp.concatenate(logit, axis=1), axis=-1)
        return _cin_forward(x, [w0, w1, w2], [b0, b1, b2])
    e = jnp.stack([tbl_0[ids[:, 0]], tbl_1[ids[:, 1]], tbl_2[ids[:, 2]], tbl_3[ids[:, 3]], tbl_4[ids[:, 4]], tbl_5[ids[:, 5]], tbl_6[ids[:, 6]], tbl_7[ids[:, 7]], tbl_8[ids[:, 8]], tbl_9[ids[:, 9]], tbl_10[ids[:, 10]], tbl_11[ids[:, 11]], tbl_12[ids[:, 12]], tbl_13[ids[:, 13]], tbl_14[ids[:, 14]], tbl_15[ids[:, 15]], tbl_16[ids[:, 16]], tbl_17[ids[:, 17]], tbl_18[ids[:, 18]], tbl_19[ids[:, 19]], tbl_20[ids[:, 20]], tbl_21[ids[:, 21]], tbl_22[ids[:, 22]], tbl_23[ids[:, 23]], tbl_24[ids[:, 24]], tbl_25[ids[:, 25]], tbl_26[ids[:, 26]], tbl_27[ids[:, 27]], tbl_28[ids[:, 28]], tbl_29[ids[:, 29]], tbl_30[ids[:, 30]], tbl_31[ids[:, 31]], tbl_32[ids[:, 32]], tbl_33[ids[:, 33]], tbl_34[ids[:, 34]], tbl_35[ids[:, 35]], tbl_36[ids[:, 36]], tbl_37[ids[:, 37]], tbl_38[ids[:, 38]]], axis=1)
    z = _L0_rec_ref(e, L0_rec_w0, L0_rec_w1, L0_rec_w2, L0_rec_b0, L0_rec_b1, L0_rec_b2)
    z = z.reshape(z.shape[0], -1)
    h = jnp.concatenate([z, dense_ctx], axis=1)
    h = jnp.maximum(h @ W_top1 + b_top1, 0.0)
    h = jnp.maximum(h @ W_top2 + b_top2, 0.0)
    y = h @ W_top3
    return y

_drawn_inputs = setup_inputs


def setup_inputs(seed=0):
    import zlib

    import numpy as np

    out = dict(_drawn_inputs(seed))
    spreads = {'b_top1': (0.0, 0.1),
     'b_top2': (0.0, 0.1),
     'L0_rec_b0': (0.0, 0.1),
     'L0_rec_b1': (0.0, 0.1),
     'L0_rec_b2': (0.0, 0.1)}
    factors = {'tbl_0': 8.0,
     'tbl_1': 8.0,
     'tbl_2': 8.0,
     'tbl_3': 8.0,
     'tbl_4': 8.0,
     'tbl_5': 8.0,
     'tbl_6': 8.0,
     'tbl_7': 8.0,
     'tbl_8': 8.0,
     'tbl_9': 8.0,
     'tbl_10': 8.0,
     'tbl_11': 8.0,
     'tbl_12': 8.0,
     'tbl_13': 8.0,
     'tbl_14': 8.0,
     'tbl_15': 8.0,
     'tbl_16': 8.0,
     'tbl_17': 8.0,
     'tbl_18': 8.0,
     'tbl_19': 8.0,
     'tbl_20': 8.0,
     'tbl_21': 8.0,
     'tbl_22': 8.0,
     'tbl_23': 8.0,
     'tbl_24': 8.0,
     'tbl_25': 8.0,
     'tbl_26': 8.0,
     'tbl_27': 8.0,
     'tbl_28': 8.0,
     'tbl_29': 8.0,
     'tbl_30': 8.0,
     'tbl_31': 8.0,
     'tbl_32': 8.0,
     'tbl_33': 8.0,
     'tbl_34': 8.0,
     'tbl_35': 8.0,
     'tbl_36': 8.0,
     'tbl_37': 8.0,
     'tbl_38': 8.0,
     'L0_rec_w0': 5.861,
     'L0_rec_w1': 8.0,
     'L0_rec_w2': 8.0}
    for name, (base, spread) in spreads.items():
        noise = np.random.default_rng([zlib.crc32(name.encode()), seed]).standard_normal(out[name].shape)
        drawn = base * np.exp(spread * noise) if base else spread * noise
        out[name] = jnp.asarray(drawn.astype(out[name].dtype))
    for name, factor in factors.items():
        out[name] = (out[name] * factor).astype(out[name].dtype)
    return out
```

```python
import numpy as np
import concourse.bass as bass
from concourse import mybir
from contextlib import ExitStack

B = 1024
M = 39
D = 16
O = 128
Q = 32
NQ = 4
R = 512
BT = R // D
NT = B // BT
NG = 9
NF = M - NQ * NG
C12 = NQ * NG + NF
C0 = NG + 1
TAIL = M - Q
HALF = TAIL // 2 + 1
XR = M + HALF - 1
BLK = 128
NB = B // BLK
TPB = BLK // BT
CTX = 16
F1, F2 = 512, 256
NH = B // R

S_FULL = NG
S_PART = S_FULL + NF
S_TB = S_PART + 1
S_TA = S_TB + 1
NS = S_TA + 1

NZ = 4
L0_CHUNKS = [[0, 1, 2], [3, 4, 5], [6, 7, 8], [9]]
L12_CHUNKS = [[NQ * g + j for j in range(NQ)] for g in range(NG)] + [[NQ * NG + f for f in range(NF)]]
N0, N12 = len(L0_CHUNKS), len(L12_CHUNKS)
STEP = N0 + 2 * N12
X_DMAS = 12
P_DMAS = NQ * NQ


def cin_tower(nc, ids, tables, ctxT, w0a, w0b, w1, w2, cin_b, wt1, wt1c, bt1, wt2, bt2, wt3, out):
    fp32, i32 = mybir.dt.float32, mybir.dt.int32
    ALU, ACT, AX = mybir.AluOpType, mybir.ActivationFunctionType, mybir.AxisListType
    with ExitStack() as ctx:
        def sb(name, shape, dt=fp32):
            return ctx.enter_context(nc.sbuf_tensor(name, shape, dt))

        def sem(name):
            return ctx.enter_context(nc.semaphore(name))

        xt = nc.dram_tensor("xt_scratch", (NT, XR, R), fp32, kind="Internal").ap()

        idx = sb("idx", [BLK, M], i32)
        emb = sb("emb", [BLK, M * D])
        X = sb("X", [128, 2, NS, R])
        Z = sb("Z", [128, NZ, NQ, R])
        PA = sb("PA", [128, NQ + 1, R])
        PB = sb("PB", [128, NQ + 1, R])
        W0 = sb("W0", [128, C0, O])
        W1 = sb("W1", [128, C12, O])
        W2 = sb("W2", [128, C12, O])
        cb = sb("cb", [128, 3])
        ones = sb("ones", [128, 128])
        WT1 = sb("WT1", [128, 3, F1])
        WT1C = sb("WT1C", [CTX, F1])
        WT2 = sb("WT2", [128, F1 // 128, F2])
        WT3 = sb("WT3", [128, F2 // 128])
        BT1 = sb("BT1", [128, F1 // 128])
        BT2 = sb("BT2", [128, F2 // 128])
        CT = sb("CT", [CTX, B])
        S = sb("S", [128, 3, B])
        H1 = sb("H1", [128, F1 // 128, R])
        H2 = sb("H2", [128, F2 // 128, R])
        Y = sb("Y", [1, B])
        ss = sb("ss", [128, 3, BT])
        sr = sb("sr", [128, 3, BT])
        root = sb("root", [128, 3, BT])
        rr = sb("rr", [128, 3, BT])
        ra = sb("ra", [128, 3, BT])
        rb = sb("rb", [128, 3, BT])
        inv = sb("inv", [128, 3, BT])

        acc = [ctx.enter_context(nc.psum_tensor(f"acc{k}", [128, R], fp32)) for k in range(3)]
        sq = [ctx.enter_context(nc.psum_tensor(f"sq{k}", [128, R], fp32)) for k in range(3)]
        nrm = [sq[k][:, 0:BT] for k in range(3)]

        idx_in = sem("idx_in")
        gathered = sem("gathered")
        xt_written = sem("xt_written")
        steps_seen = sem("steps_seen")
        tiles_there = sem("tiles_there")
        x_loaded = [sem("x_loaded0"), sem("x_loaded1")]
        w0_in, w1_in, w2_in, wt_in = sem("w0_in"), sem("w1_in"), sem("w2_in"), sem("wt_in")
        w0_ready = sem("w0_ready")
        ones_ready = sem("ones_ready")
        z_ready = sem("z_ready")
        z_used = sem("z_used")
        raw = [sem(f"raw{k}") for k in range(3)]
        acc_free = [sem(f"acc_free{k}") for k in range(3)]
        biased = [sem(f"biased{k}") for k in range(3)]
        scaled2 = sem("scaled2")
        squared = [sem(f"squared{k}") for k in range(3)]
        summed = [sem(f"summed{k}") for k in range(3)]
        norm2 = [sem(f"norm2_{k}") for k in range(3)]
        rooted = [sem(f"rooted{k}") for k in range(3)]
        p0_ready = sem("p0_ready")
        pa_in, pb_in = sem("pa_in"), sem("pb_in")
        s_ready = sem("s_ready")
        chain = sem("chain")
        top_ready = sem("top_ready")
        top_used = sem("top_used")
        y_out = sem("y_out")

        block = ctx.enter_context(nc.Block())

        def bc_d(a):
            return a.unsqueeze(2).to_broadcast([128, BT, D])

        def bd(a):
            return a.rearrange("p (b d) -> p b d", d=D)

        def base(t):
            return STEP * t - N12

        @block.gpsimd
        def _(pool):
            with pool.Fori(0, NB) as n:
                pool.dma_start(idx[:], ids[bass.ds(n * BLK, BLK), :]).then_inc(idx_in, 16)
                pool.wait_ge(idx_in, 16 * n + 16)
                pool.sem_inc(steps_seen, 1)
                for f in range(M):
                    nc.gpsimd.indirect_dma_start(
                        out=emb[:, f * D:(f + 1) * D], out_offset=None, in_=tables[f],
                        in_offset=bass.IndirectOffsetOnAxis(ap=idx[:, f:f + 1], axis=0),
                    ).then_inc(gathered, 16)
                pool.wait_ge(gathered, 16 * M * n + 16 * M)
                pool.sem_inc(steps_seen, 1)
                for k in range(TPB):
                    at = (n * TPB + k) * (XR * R)
                    e = emb[k * BT:(k + 1) * BT, :].rearrange("b (m d) -> b m d", d=D)
                    pool.dma_start(bass.AP(xt.tensor, at, [[D, BT], [R, M], [1, D]]), e).then_inc(xt_written, 16)
                    pool.dma_start(bass.AP(xt.tensor, at + M * R, [[D, BT], [R, XR - M], [1, D]]),
                                   e[:, Q:Q + XR - M, :]).then_inc(xt_written, 16)
                pool.wait_ge(xt_written, 32 * TPB * n + 32 * TPB)
                pool.sem_inc(tiles_there, TPB)

        def load_x(sp, t, par):
            at = t * (XR * R)

            def src(row, ap):
                return bass.AP(xt.tensor, at + row * R, ap)

            def load(dst, s):
                sp.dma_start(dst, s).then_inc(x_loaded[par], 16)

            Xp = X[:, par, :, :]
            for q in range(NQ):
                load(Xp[Q * q:Q * q + Q, S_PART:S_PART + (2 if q < 3 else 1), :],
                     src(0, [[R, Q], [0, 2], [1, R]] if q < 3 else [[R, Q], [1, R]]))
                load(Xp[Q * q:Q * q + Q, 0:NG, :], src(q, [[0, Q], [NQ * R, NG], [1, R]]))
            load(Xp[0:Q * NF, S_TA, :], src(Q + NQ, [[R, NF], [0, Q], [1, R]]))
            load(Xp[Q * NF:Q * NF + HALF * TAIL, S_TA, :], src(Q, [[0, HALF], [R, TAIL], [1, R]]))
            load(Xp[Q * NF:Q * NF + HALF * TAIL, S_TB, :], src(Q, [[R, HALF], [R, TAIL], [1, R]]))
            load(Xp[:, S_FULL:S_FULL + NF, :], src(Q + NQ, [[0, 128], [1, NF * R]]))

        def spread(sp, P, arrived):
            for j in range(NQ):
                for q in range(NQ):
                    sp.dma_start(P[Q * q:Q * q + Q, j, :], P[Q * j:Q * j + Q, NQ, :]).then_inc(arrived, 16)

        @block.sync
        def _(sp):
            def step(t, par, more=True):
                sp.wait_ge(p0_ready, t + 1)
                spread(sp, PA, pa_in)
                if more:
                    sp.wait_ge(tiles_there, t + 2)
                    sp.wait_ge(z_ready, base(t) + N0 + N12)
                    load_x(sp, t + 1, 1 - par)
                sp.wait_ge(biased[1], t + 1)
                spread(sp, PB, pb_in)

            sp.wait_ge(tiles_there, 1)
            sp.wait_ge(ones_ready, 1)
            load_x(sp, 0, 0)
            sp.wait_ge(tiles_there, 2)
            load_x(sp, 1, 1)
            sp.wait_ge(p0_ready, 1)
            spread(sp, PA, pa_in)
            sp.wait_ge(biased[1], 1)
            spread(sp, PB, pb_in)
            with sp.Fori(0, (NT - 2) // 2) as i:
                step(2 * i + 1, 1)
                step(2 * i + 2, 0)
            step(NT - 1, 1, more=False)
            sp.wait_ge(top_used, NH * (F1 // 128 + F2 // 128 + 1))
            sp.dma_start(out, Y[:]).then_inc(y_out, 16)
            sp.wait_ge(y_out, 16)

        @block.scalar
        def _(act):
            def load(dst, src, s):
                act.dma_start(dst, src).then_inc(s, 16)

            ZA = Z[:, :, :, :].rearrange("p a b c -> p (a b c)")
            load(ZA[:, 0:C0 * O], w0a, w0_in)
            load(ZA[:, C0 * O:2 * C0 * O], w0b, w0_in)
            load(cb[:], cin_b, w0_in)
            load(W1[:].rearrange("p c o -> p (c o)"), w1, w1_in)
            load(W2[:].rearrange("p c o -> p (c o)"), w2, w2_in)
            for dst, src in ((WT1[:], wt1), (WT1C[:], wt1c), (WT2[:], wt2), (WT3[:], wt3),
                             (BT1[:], bt1), (BT2[:], bt2), (CT[:], ctxT)):
                load(dst, src, wt_in)
            act.wait_ge(w0_in, 48)

            def bias0(t):
                act.wait_ge(raw[0], t + 1)
                nc.scalar.activation(acc[0][:], acc[0][:], ACT.Identity, bias=cb[:, 0:1]).then_inc(biased[0], 1)
                act.wait_ge(biased[0], t + 1)
                nc.scalar.activation(sq[0][:], acc[0][:], ACT.Square).then_inc(squared[0], 1)

            def bias1(t, z_done):
                act.wait_ge(raw[1], t + 1)
                if z_done is not None:
                    act.wait_ge(z_ready, z_done)
                    act.wait_ge(pb_in, 16 * P_DMAS * t)
                nc.scalar.activation(PB[:, NQ, :], acc[1][:], ACT.Identity, bias=cb[:, 1:2]).then_inc(biased[1], 1)
                act.wait_ge(biased[1], t + 1)
                nc.scalar.activation(sq[1][:], PB[:, NQ, :], ACT.Square).then_inc(squared[1], 1)

            def bias2(t):
                act.wait_ge(scaled2, t + 1)
                nc.scalar.activation(acc[2][:], acc[2][:], ACT.Identity, bias=cb[:, 2:3]).then_inc(biased[2], 1)
                act.wait_ge(biased[2], t + 1)
                nc.scalar.activation(sq[2][:], acc[2][:], ACT.Square).then_inc(squared[2], 1)

            def take_root(k, t):
                act.wait_ge(norm2[k], t + 1)
                nc.scalar.activation(root[:, k, :], nrm[k], ACT.Sqrt).then_inc(rooted[k], 1)

            def step(t):
                bias0(t)
                take_root(1, t - 1)
                take_root(0, t)
                bias2(t - 1)
                take_root(2, t - 1)
                bias1(t, base(t) + N0 + N12)

            bias0(0)
            take_root(0, 0)
            bias1(0, None)
            with act.Fori(0, (NT - 2) // 2) as i:
                step(2 * i + 1)
                step(2 * i + 2)
            step(NT - 1)
            take_root(1, NT - 1)
            bias2(NT - 1)
            take_root(2, NT - 1)

            act.wait_ge(wt_in, 16 * 7)
            n = 0
            for half in range(NH):
                for H, bias, blocks in ((H1, BT1, F1 // 128), (H2, BT2, F2 // 128)):
                    for o in range(blocks):
                        n += 1
                        act.wait_ge(top_ready, n)
                        nc.scalar.activation(H[:, o, :], acc[n % 3][:], ACT.Relu,
                                             bias=bias[:, o:o + 1]).then_inc(top_used, 1)
                n += 1
                act.wait_ge(top_ready, n)
                nc.scalar.copy(Y[0:1, half * R:half * R + R], acc[n % 3][0:1, :]).then_inc(top_used, 1)

        @block.vector
        def _(dve):
            nc.vector.memset(X[Q * NF:128, :, S_TB:S_TA + 1, :], 0.0).then_inc(chain, 1)
            dve.wait_ge(chain, 1)
            nc.vector.memset(ones[:], 1.0).then_inc(ones_ready, 1)
            dve.wait_ge(w0_in, 48)
            ZA = Z[:, :, :, :].rearrange("p a b c -> p (a b c)")
            nc.vector.tensor_tensor(W0[:].rearrange("p c o -> p (c o)"), ZA[:, 0:C0 * O], ZA[:, C0 * O:2 * C0 * O],
                                    ALU.add).then_inc(w0_ready, 1)
            dve.wait_ge(w0_ready, 1)
            LINK = 4

            bufs = [0]

            def next_buffer(pos):
                if not (isinstance(pos, int) and pos < NZ):
                    dve.wait_ge(z_used, pos - NZ + 1)
                bufs[0] += 1
                return (bufs[0] - 1) % NZ

            def form0(c, pos, par):
                buf = next_buffer(pos)
                Xp = X[:, par, :, :]
                ks = L0_CHUNKS[c]
                n = len(ks)
                if ks[0] < NG:
                    a, b = Xp[:, ks[0]:ks[0] + n, :], Xp[:, S_PART:S_PART + 1, :].to_broadcast([128, n, R])
                else:
                    a, b = Xp[:, S_TA:S_TA + 1, :], Xp[:, S_TB:S_TB + 1, :]
                nc.vector.tensor_tensor(Z[:, buf, 0:n, :], a, b, ALU.mult).then_inc(z_ready, 1)

            def form12(P, c, pos, par):
                buf = next_buffer(pos)
                Xp = X[:, par, :, :]
                if c < NG:
                    a, b, n = P[:, 0:NQ, :], Xp[:, c:c + 1, :].to_broadcast([128, NQ, R]), NQ
                else:
                    a, b, n = P[:, NQ:NQ + 1, :].to_broadcast([128, NF, R]), Xp[:, S_FULL:S_FULL + NF, :], NF
                nc.vector.tensor_tensor(Z[:, buf, 0:n, :], a, b, ALU.mult).then_inc(z_ready, 1)

            def reduce(k, t, src):
                dve.wait_ge(squared[k], t + 1)
                nc.vector.reduce_sum(sr[:, k, :], bd(src), axis=AX.X)
                nc.vector.reduce_sum(ss[:, k, :], bd(sq[k][:]), axis=AX.X).then_inc(summed[k], 1)

            def invert(k, t, n):
                def link(ins, m):
                    ins.then_inc(chain, 1)
                    dve.wait_ge(chain, n + m)

                dve.wait_ge(rooted[k], t + 1)
                link(nc.vector.reciprocal(rr[:, k, :], root[:, k, :]), 1)
                link(nc.vector.scalar_tensor_tensor(ra[:, k, :], rr[:, k, :], -0.5, nrm[k], ALU.mult, ALU.mult), 2)
                link(nc.vector.tensor_tensor(rb[:, k, :], ra[:, k, :], rr[:, k, :], ALU.mult), 3)
                link(nc.vector.scalar_tensor_tensor(inv[:, k, :], rb[:, k, :], 1.5, rr[:, k, :], ALU.add, ALU.mult), 4)

            def keep_sums(k, t):
                return nc.vector.tensor_tensor(S[:, k, bass.ds(t * BT, BT)], sr[:, k, :], inv[:, k, :], ALU.mult)

            def norm0(t, n, pa_read):
                invert(0, t, n)
                keep_sums(0, t)
                if pa_read:
                    dve.wait_ge(pa_in, 16 * P_DMAS * t)
                nc.vector.tensor_tensor(bd(PA[:, NQ, :]), bd(acc[0][:]), bc_d(inv[:, 0, :]),
                                        ALU.mult).then_inc(p0_ready, 1)

            def scale2(t):
                dve.wait_ge(raw[2], t + 1)
                nc.vector.tensor_tensor(bd(acc[2][:]), bd(acc[2][:]), bc_d(inv[:, 1, :]), ALU.mult).then_inc(scaled2, 1)

            def layer1(t, at, par, n):
                dve.wait_ge(pa_in, 16 * P_DMAS * (t + 1))
                for c in range(N12):
                    form12(PA, c, at + c, par)
                    if n is None:
                        continue
                    if c == 4:
                        scale2(t - 1)
                    if c == 6:
                        reduce(2, t - 1, acc[2][:])
                    if c == 9:
                        invert(2, t - 1, n)
                        keep_sums(2, t - 1)

            dve.wait_ge(x_loaded[0], 16 * X_DMAS)
            for c in range(N0):
                form0(c, c, 0)
            reduce(0, 0, acc[0][:])
            norm0(0, 1, False)
            layer1(0, N0, 0, None)

            def step(t, par, loads):
                at = base(t)
                n = 1 + LINK + 3 * LINK * (t - 1)
                dve.wait_ge(x_loaded[par], loads * 16 * X_DMAS)
                for c in range(N0):
                    form0(c, at + c, par)
                dve.wait_ge(pb_in, 16 * P_DMAS * t)
                for c in range(N12):
                    form12(PB, c, at + N0 + c, 1 - par)
                    if c == 1:
                        reduce(1, t - 1, PB[:, NQ, :])
                        reduce(0, t, acc[0][:])
                    if c == 6:
                        invert(1, t - 1, n)
                        keep_sums(1, t - 1)
                        norm0(t, n + LINK, True)
                layer1(t, at + N0 + N12, par, n + 2 * LINK)

            with dve.Fori(0, (NT - 2) // 2) as i:
                step(2 * i + 1, 1, i + 1)
                step(2 * i + 2, 0, i + 2)
            step(NT - 1, 1, NT // 2)

            last = NT - 1
            n = 1 + LINK + 3 * LINK * last
            dve.wait_ge(pb_in, 16 * P_DMAS * NT)
            for c in range(N12):
                form12(PB, c, base(NT) + c, 1)
                if c == 1:
                    reduce(1, last, PB[:, NQ, :])
                if c == 6:
                    invert(1, last, n)
                    keep_sums(1, last)
            scale2(last)
            reduce(2, last, acc[2][:])
            invert(2, last, n + LINK)
            keep_sums(2, last).then_inc(s_ready, 1)

        @block.tensor
        def _(pe):
            bufs = [0]

            def products(W, k, chunks, at, after=None, between=()):
                nblocks = sum(map(len, chunks))
                for c, ks in enumerate(chunks):
                    pe.wait_ge(z_ready, at + c + 1)
                    for j, b in enumerate(ks):
                        last = nc.tensor.matmul(acc[k][:], W[:, b, :], Z[:, bufs[0] % NZ, j, :],
                                                start=(b == 0), stop=(b == nblocks - 1))
                    bufs[0] += 1
                    last.then_inc(z_used, 1)
                    if c == len(chunks) - 1:
                        continue
                    for at_c, work in between:
                        if at_c == c:
                            work()
                pe.wait_ge(z_used, at + len(chunks))
                pe.sem_inc(raw[k], 1)

            def norm(k, t):
                pe.wait_ge(summed[k], t + 1)
                nc.tensor.matmul(nrm[k], ones[:], ss[:, k, :], start=True, stop=True).then_inc(norm2[k], 1)

            pe.wait_ge(ones_ready, 1)
            pe.wait_ge(w0_ready, 1)
            products(W0, 0, L0_CHUNKS, 0)
            norm(0, 0)
            pe.wait_ge(w1_in, 16)
            products(W1, 1, L12_CHUNKS, N0)
            pe.wait_ge(w2_in, 16)

            def step(t, first=False):
                at = base(t)
                pe.wait_ge(p0_ready, t)
                products(W0, 0, L0_CHUNKS, at)
                products(W2, 2, L12_CHUNKS, at + N0, between=((3, lambda: norm(1, t - 1)), (4, lambda: norm(0, t))))
                pe.wait_ge(biased[1], t)
                products(W1, 1, L12_CHUNKS, at + N0 + N12, between=((7, lambda: norm(2, t - 1)),))

            with pe.Fori(0, (NT - 2) // 2) as i:
                step(2 * i + 1)
                step(2 * i + 2)
            step(NT - 1)
            products(W2, 2, L12_CHUNKS, base(NT), between=((3, lambda: norm(1, NT - 1)),))
            norm(2, NT - 1)

            pe.wait_ge(wt_in, 16 * 7)
            pe.wait_ge(s_ready, 1)
            n = 0
            for half in range(NH):
                cols = slice(half * R, half * R + R)

                def bank():
                    if n > 3:
                        pe.wait_ge(top_used, n - 3)
                    return acc[n % 3]

                for o in range(F1 // 128):
                    n += 1
                    a, u = bank(), slice(o * 128, o * 128 + 128)
                    for k in range(3):
                        nc.tensor.matmul(a[:], WT1[:, k, u], S[:, k, cols], start=(k == 0), stop=False)
                    nc.tensor.matmul(a[:], WT1C[:, u], CT[:, cols], start=False, stop=True).then_inc(top_ready, 1)
                pe.wait_ge(top_used, n)
                for o in range(F2 // 128):
                    n += 1
                    a = bank()
                    for k in range(F1 // 128):
                        last = nc.tensor.matmul(a[:], WT2[:, k, o * 128:o * 128 + 128], H1[:, k, :],
                                                start=(k == 0), stop=(k == F1 // 128 - 1))
                    last.then_inc(top_ready, 1)
                pe.wait_ge(top_used, n)
                n += 1
                a = bank()
                for k in range(F2 // 128):
                    last = nc.tensor.matmul(a[0:1, :], WT3[:, k:k + 1], H2[:, k, :],
                                            start=(k == 0), stop=(k == F2 // 128 - 1))
                last.then_inc(top_ready, 1)


def layer0_rows():
    a = np.full((C0, 128), M * M)
    b = np.full((C0, 128), M * M)

    def put(block, p, m, h):
        a[block, p] = m * M + h
        if m != h:
            b[block, p] = h * M + m

    for m in range(NQ * NG):
        for h in range(min(m + 1, Q)):
            put(m // NQ, (m % NQ) * Q + h, m, h)
    for f in range(NF):
        for h in range(Q):
            put(NG, f * Q + h, NQ * NG + f, h)
    for k in range(HALF):
        for m in range(TAIL):
            put(NG, NF * Q + k * TAIL + m, Q + m, Q + (m + k) % TAIL)
    return a, b


def layer12_rows():
    r = np.empty((C12, 128), np.int64)
    p = np.arange(128)
    for g in range(NG):
        for j in range(NQ):
            r[NQ * g + j] = (NQ * g + p // Q) * O + Q * j + p % Q
    for f in range(NF):
        r[NQ * NG + f] = (NQ * NG + f) * O + p
    return r


def kernel(**inputs):
    import concourse.bacc as bacc
    from concourse.bass_utils import run_bass_kernel_spmd

    given = {k: np.asarray(v) for k, v in inputs.items()}

    def blocks(w, rows):
        return w[rows].transpose(1, 0, 2).reshape(128, -1)

    a0, b0 = layer0_rows()
    w0 = np.concatenate([given["L0_rec_w0"], np.zeros((1, O), given["L0_rec_w0"].dtype)])
    r12 = layer12_rows()
    wt1, wt2 = given["W_top1"], given["W_top2"]
    arrays = {
        "ids": given["ids"],
        **{f"tbl_{f}": given[f"tbl_{f}"] for f in range(M)},
        "ctxT": given["dense_ctx"].T,
        "w0a": blocks(w0, a0), "w0b": blocks(w0, b0),
        "w1": blocks(given["L0_rec_w1"], r12), "w2": blocks(given["L0_rec_w2"], r12),
        "cin_b": np.stack([given[f"L0_rec_b{k}"] for k in range(3)], axis=1),
        "wt1": wt1[:3 * O].reshape(3, O, F1).transpose(1, 0, 2), "wt1c": wt1[3 * O:],
        "bt1": given["b_top1"].reshape(-1, 128).T,
        "wt2": wt2.reshape(F1 // 128, 128, F2).transpose(1, 0, 2),
        "bt2": given["b_top2"].reshape(-1, 128).T,
        "wt3": given["W_top3"].reshape(F2 // 128, 128).T,
    }
    arrays = {f"in_{k}": np.ascontiguousarray(v) for k, v in arrays.items()}
    nc = bacc.Bacc("TRN2", target_bir_lowering=False, num_devices=1)
    ap = {k[3:]: nc.dram_tensor(k, v.shape, mybir.dt.from_np(v.dtype), kind="ExternalInput").ap()
          for k, v in arrays.items()}
    out = nc.dram_tensor("out_y", (1, B), mybir.dt.float32, kind="ExternalOutput").ap()
    cin_tower(nc, ap["ids"], [ap[f"tbl_{f}"] for f in range(M)], ap["ctxT"], ap["w0a"], ap["w0b"], ap["w1"],
              ap["w2"], ap["cin_b"], ap["wt1"], ap["wt1c"], ap["bt1"], ap["wt2"], ap["bt2"], ap["wt3"], out)
    r = run_bass_kernel_spmd(nc, [arrays], core_ids=[0])
    return r.results[0]["out_y"].reshape(B, 1)
```

```python
import numpy as np
import concourse.bass as bass
from concourse import mybir
from contextlib import ExitStack

B = 1024
M = 39
D = 16
O = 128
Q = 32
NQ = 4
R = 512
BT = R // D
NT = B // BT
NG = 9
NF = M - NQ * NG
C12 = NQ * NG + NF
C0 = NG + 1
TAIL = M - Q
HALF = TAIL // 2 + 1
XR = M + HALF - 1
BLK = 128
NB = B // BLK
TPB = BLK // BT
CTX = 16
F1, F2 = 512, 256
NH = B // R

S_FULL = NG
NS = S_FULL + NF
T_PART, T_B, T_A = range(3)
NT0 = 3

WIDE = 3
NZ = 5
NZH = 3
NZL = 3
NPJ = 2

MODES = {0: "VGFF", 1: "FGFGFGVGFGFGG", 2: "FFGGFGVGFGFGG"}
SPREADS = "sabcd"


class Chunk:

    def __init__(self, layer, c):
        self.layer, self.c, self.mode = layer, c, MODES[layer][c]
        if layer == 0:
            self.blocks = list(range(WIDE * c, min(WIDE * c + WIDE, C0)))
            self.spread = "s" if c < NG // WIDE else None
        elif c == 0:
            self.blocks = [NQ * NG + f for f in range(NF)]
            self.spread = None
        else:
            j, g = divmod(c - 1, NG // WIDE)
            self.blocks = [NQ * (g * WIDE + k) + j for k in range(WIDE)]
            self.slots = slice(g * WIDE, g * WIDE + WIDE)
            self.spread = SPREADS[1 + j]
        self.first, self.last = c == 0, c == len(MODES[layer]) - 1


def layer_chunks(layer):
    return [Chunk(layer, c) for c in range(len(MODES[layer]))]


class Part:

    def __init__(self, t):
        self.t = t
        static = isinstance(t, int)
        self.kind = "first" if static and t == 0 else "last" if static and t == NT else "middle"
        layers = {"first": [0, 1], "middle": [0, 2, 1], "last": [2]}[self.kind]
        self.chunks = [k for layer in layers for k in layer_chunks(layer)]
        self.before = [] if self.kind == "first" else layer_chunks(1)

    def count(self, what, r=0, at=None):
        t = self.t if at is None else at
        inside = self.before + self.chunks
        n = len(self.before)
        rel = sum(map(what, inside[n:n + r])) if r >= 0 else -sum(map(what, inside[n + r:n]))
        if self.kind == "first":
            return rel
        head = sum(map(what, layer_chunks(0) + layer_chunks(1)))
        every = head + sum(map(what, layer_chunks(2)))
        return t * every + (head - every + rel)

    def buffer(self, what, r, ring, like):
        return self.count(what, r, at=like) % ring

    def back(self, what, r, n):
        inside = self.before + self.chunks
        found = [k for k in range(len(self.before) + r) if what(inside[k])]
        if len(found) < n:
            assert self.kind == "first"
            return None
        return found[-n] - len(self.before)

    def get(self, r):
        inside = self.before + self.chunks
        k = r + len(self.before)
        return inside[k] if k >= 0 else None


def every(k):
    return 1


def split(k):
    return int(k.mode in "VG")


def by_vector(k):
    return int(k.mode == "V")


def by_pool(k):
    return int(k.mode == "G")


def starts_spread(k):
    return int(k.spread is not None and (k.c == (0 if k.layer == 0 else 1) or (k.layer and (k.c - 1) % (NG // WIDE) == 0)))


_two = 2 * [k for layer in range(3) for k in layer_chunks(layer)]
for _what, _ring in ((every, NZ), (split, NZH), (split, NZL), (starts_spread, NPJ)):
    assert sum(map(_what, _two)) % _ring == 0

SLOT_F, SLOT_S = {}, {}
for _layer in range(3):
    for _k in layer_chunks(_layer):
        for _b in _k.blocks:
            _s = SLOT_S if split(_k) else SLOT_F
            _s[_layer, _b] = len(_s)
NWF, NWS = len(SLOT_F), len(SLOT_S)
NF0, NS0 = (sum(k[0] == 0 for k in s) for s in (SLOT_F, SLOT_S))
LAG = 2
TOP_SPLIT = F1 // 128
TOP = F1 // 128 + F2 // 128 + 1


def cin_tower(nc, ids, tables, ctxT, w0a, w0b, wf, ws, cin_b, wt1, wt1c, bt1, wt2, bt2, wt3, out):
    fp32, fp32r, i32 = mybir.dt.float32, mybir.dt.float32r, mybir.dt.int32
    ALU, ACT, AX = mybir.AluOpType, mybir.ActivationFunctionType, mybir.AxisListType
    with ExitStack() as ctx:
        def sb(name, shape, dt=fp32):
            return ctx.enter_context(nc.sbuf_tensor(name, shape, dt))

        def sem(name):
            return ctx.enter_context(nc.semaphore(name))

        xt = nc.dram_tensor("xt_scratch", (NT, XR, R), fp32, kind="Internal").ap()
        S_all = nc.dram_tensor("sums_scratch", (3, O, B), fp32, kind="Internal").ap()

        idx = sb("idx", [BLK, M], i32)
        emb = sb("emb", [BLK, M * D])
        X = sb("X", [128, 2, NS, R])
        X0 = sb("X0", [128, NT0, R])
        Z = sb("Z", [128, NZ, WIDE, R])
        ZH = sb("ZH", [128, NZH, WIDE, R], fp32r)
        ZL = sb("ZL", [128, NZL, WIDE, R], fp32r)
        PA = sb("PA", [128, R])
        PB = sb("PB", [128, R])
        WF = sb("WF", [128, NWF, O])
        WH = sb("WH", [128, NWS, O], fp32r)
        WL = sb("WL", [128, NWS, O], fp32r)
        cb = sb("cb", [128, 3])
        ones = sb("ones", [128, 128])
        WT3 = sb("WT3", [128, F2 // 128])
        BT1 = sb("BT1", [128, F1 // 128])
        BT2 = sb("BT2", [128, F2 // 128])
        sums = sb("sums", [128, 2, 3, BT])
        ss = sb("ss", [128, 3, BT])
        sr = sb("sr", [128, 3, BT])
        root = sb("root", [128, 3, BT])
        rr = sb("rr", [128, 3, BT])
        ra = sb("ra", [128, 3, BT])
        rb = sb("rb", [128, 3, BT])
        inv = sb("inv", [128, 3, BT])
        ZHf, ZLf = ZH[:].bitcast(fp32), ZL[:].bitcast(fp32)

        Xtop = X[:, 0, :, :].rearrange("p s r -> p (s r)")
        cut = np.cumsum([0, 3 * F1, F1, F1 // 128 * F2, B, F1 // 128 * R])
        WT1 = Xtop[:, cut[0]:cut[1]].rearrange("p (k n) -> p k n", k=3)
        WT1C = Xtop[0:CTX, cut[1]:cut[2]]
        WT2 = Xtop[:, cut[2]:cut[3]].rearrange("p (k n) -> p k n", n=F2)
        CT = Xtop[0:CTX, cut[3]:cut[4]]
        H1 = Xtop[:, cut[4]:cut[5]].rearrange("p (k n) -> p k n", n=R)
        S = X[:, 1, 0:3 * B // R, :].rearrange("p s r -> p (s r)").rearrange("p (k b) -> p k b", k=3)
        Zall = Z[:].rearrange("p a b c -> p (a b c)")
        H2 = Zall[:, 0:F2 // 128 * R].rearrange("p (k n) -> p k n", n=R)
        Y = Zall[0:1, F2 // 128 * R:F2 // 128 * R + B]

        Xodd = X[:, 1, :, :].rearrange("p s r -> p (s r)")
        W0A, W0B = Xodd[:, 0:C0 * O], Xodd[:, C0 * O:2 * C0 * O]
        NWB = NWS - NS0
        half = NWB // 2 * O
        WSA, WSB = Zall[:, 0:half], Xodd[:, 2 * C0 * O:2 * C0 * O + NWB * O - half]

        def bank(name):
            return ctx.enter_context(nc.psum_tensor(name, [128, R], fp32))

        acc = [bank(f"acc{k}") for k in range(3)]
        sq = [bank(f"sq{k}") for k in range(3)]
        PJ = [bank(f"PJ{k}") for k in range(NPJ)]
        TB = [acc[0], acc[1], PJ[0]]
        nrm = [sq[k][:, 0:BT] for k in range(3)]

        idx_in = sem("idx_in")
        gathered = sem("gathered")
        xt_written = sem("xt_written")
        steps_seen = sem("steps_seen")
        x_loaded = [sem("x_loaded_even"), sem("x_loaded_odd")]
        x0_loaded = sem("x0_loaded")
        w0_in, ws_in, wf_in, wt_in = sem("w0_in"), sem("ws_in"), sem("wf_in"), sem("wt_in")
        w0_folded = sem("w0_folded")
        wh_ready = sem("wh_ready")
        w_ready = sem("w_ready")
        ones_ready = sem("ones_ready")
        spread_ready = sem("spread_ready")
        z_ready = sem("z_ready")
        zh_ready = sem("zh_ready")
        zl_vector = sem("zl_vector")
        zl_pool = sem("zl_pool")
        used = sem("used")
        raw = [sem(f"raw{k}") for k in range(3)]
        biased = [sem(f"biased{k}") for k in range(3)]
        scaled2 = sem("scaled2")
        squared = [sem(f"squared{k}") for k in range(3)]
        summed = [sem(f"summed{k}") for k in range(3)]
        norm2 = [sem(f"norm2_{k}") for k in range(3)]
        rooted = [sem(f"rooted{k}") for k in range(3)]
        p0_ready = sem("p0_ready")
        sums_ready = [sem(f"sums_ready{k}") for k in range(3)]
        sums_out = [sem(f"sums_out{k}") for k in range(3)]
        s_in = [sem(f"s_in{h}") for h in range(NH)]
        chain = sem("chain")
        top_ready = sem("top_ready")
        top_used = sem("top_used")
        y_out = sem("y_out")

        block = ctx.enter_context(nc.Block())

        def bc_d(a):
            return a.unsqueeze(2).to_broadcast([128, BT, D])

        def bd(a):
            return a.rearrange("p (b d) -> p b d", d=D)

        @block.gpsimd
        def _(pool):
            def gather(fields):
                for f in fields:
                    nc.gpsimd.indirect_dma_start(
                        out=emb[:, f * D:(f + 1) * D], out_offset=None, in_=tables[f],
                        in_offset=bass.IndirectOffsetOnAxis(ap=idx[:, f:f + 1], axis=0),
                    ).then_inc(gathered, 16)

            def step(t, like, between=()):
                part = Part(t)
                between = dict(between)
                for r, k in enumerate(part.chunks):
                    if not by_pool(k):
                        continue
                    pool.wait_ge(zh_ready, part.count(split, r) + 1)
                    old = part.back(split, r, NZL)
                    if old is not None:
                        pool.wait_ge(used, part.count(every, old) + 1)
                    n = len(k.blocks)
                    z = Z[:, part.buffer(every, r, NZ, like), 0:n, :]
                    zh = ZHf[:, part.buffer(split, r, NZH, like), 0:n, :]
                    zl = ZL[:, part.buffer(split, r, NZL, like), 0:n, :]
                    nc.gpsimd.tensor_tensor(zl, z, zh, ALU.subtract).then_inc(zl_pool, 1)
                    work = between.pop(sum(map(by_pool, part.chunks[:r])), None)
                    if work:
                        work()

            nper = sum(map(by_pool, Part(1).chunks))
            thirds = [range(M * k // 3, M * (k + 1) // 3) for k in range(3)]

            def lookups(k, slots):
                fields = list(thirds[k])
                cuts = [fields[len(fields) * i // slots:len(fields) * (i + 1) // slots] for i in range(slots)]
                return [(i, lambda g=g: gather(g)) for i, g in enumerate(cuts) if g]

            def four(t):
                n = (t // TPB if isinstance(t, int) else t[0]) + 1
                at = t if isinstance(t, int) else t[0] * TPB
                pool.wait_ge(idx_in, 16 * n + 16)
                pool.sem_inc(steps_seen, 1)
                pool.wait_ge(xt_written, 32 * TPB * n)
                pool.sem_inc(steps_seen, 1)
                for k in range(3):
                    like = 0 if isinstance(t, int) and k == 0 else 1 + (k + 1) % 2
                    slots = sum(map(by_pool, Part(0).chunks)) if like == 0 else nper
                    step(at + k, like, lookups(k, slots))
                step(at + 3, 1)

            pool.wait_ge(idx_in, 16)
            gather(range(M))
            four(0)
            with pool.Fori(1, NB - 1) as i:
                four((i,))
            for t in range(TPB * (NB - 1), NT + 1):
                step(t, 1 + (t + 1) % 2)

        @block.sync
        def _(sp):
            def source(t, row, ap):
                return bass.AP(xt.tensor, t * (XR * R) + row * R, ap)

            def load_x(t, par):
                for q in range(NQ):
                    sp.dma_start(X[Q * q:Q * q + Q, par, 0:NG, :],
                                 source(t, q, [[0, Q], [NQ * R, NG], [1, R]])).then_inc(x_loaded[par], 16)
                sp.dma_start(X[:, par, S_FULL:NS, :],
                             source(t, NQ * NG, [[0, 128], [1, NF * R]])).then_inc(x_loaded[par], 16)

            def load_x0(t):
                for q in range(NQ):
                    slots = slice(T_PART, T_B + 1) if q < NF else slice(T_PART, T_PART + 1)
                    ap = [[R, Q], [0, 2], [1, R]] if q < NF else [[R, Q], [1, R]]
                    sp.dma_start(X0[Q * q:Q * q + Q, slots, :], source(t, 0, ap)).then_inc(x0_loaded, 16)
                rest = slice(Q * NF, Q * NF + HALF * TAIL)
                for dst, src in ((X0[0:Q * NF, T_A, :], source(t, NQ * NG, [[R, NF], [0, Q], [1, R]])),
                                 (X0[rest, T_A, :], source(t, Q, [[0, HALF], [R, TAIL], [1, R]])),
                                 (X0[rest, T_B, :], source(t, Q, [[R, HALF], [R, TAIL], [1, R]]))):
                    sp.dma_start(dst, src).then_inc(x0_loaded, 16)

            def fetch_indices(n):
                sp.dma_start(idx[:], ids[bass.ds(n * BLK, BLK), :]).then_inc(idx_in, 16)

            def write_tiles(n, ks):
                for k in ks:
                    at = (n * TPB + k) * (XR * R)
                    e = emb[k * BT:(k + 1) * BT, :].rearrange("b (m d) -> b m d", d=D)
                    sp.dma_start(bass.AP(xt.tensor, at, [[D, BT], [R, M], [1, D]]), e).then_inc(xt_written, 16)
                    sp.dma_start(bass.AP(xt.tensor, at + M * R, [[D, BT], [R, XR - M], [1, D]]),
                                 e[:, Q:Q + XR - M, :]).then_inc(xt_written, 16)

            def save_sums(k, t, par, before=True):
                sp.wait_ge(sums_ready[k], t + 1)
                sp.dma_start(S_all[k, :, bass.ds(t * BT, BT)], sums[:, par, k, :]).then_inc(sums_out[k], 16)

            def load_sums(h):
                sp.dma_start(S[:, :, h * R:h * R + R],
                             S_all[:, :, h * R:h * R + R].rearrange("k p b -> p k b")).then_inc(s_in[h], 16)

            def step(t, par, block=None, more=True):
                part = Part(t)
                n0 = len(MODES[0])
                for k, n in ((0, t), (1, t - 1), (2, t - 1)):
                    if not isinstance(t, int) or n > 0:
                        sp.wait_ge(sums_out[k], 16 * n)
                if block is not None:
                    sp.wait_ge(gathered, 16 * M * block + 16 * M)
                    write_tiles(block, range(TPB))
                    sp.wait_ge(xt_written, 32 * TPB * block + 32 * TPB)
                if more:
                    sp.wait_ge(z_ready, part.count(every, n0))
                    load_x0(t + 1)
                if part.kind == "first":
                    sp.wait_ge(w_ready, 3)
                    load_x(1, 1)
                elif more:
                    sp.wait_ge(z_ready, part.count(every, n0 + len(MODES[2])))
                    load_x(t + 1, 1 - par)
                if part.kind != "first":
                    save_sums(1, t - 1, 1 - par)
                save_sums(0, t, par)
                if part.kind != "first":
                    save_sums(2, t - 1, 1 - par)

            fetch_indices(0)
            sp.wait_ge(gathered, 16 * M)
            write_tiles(0, [0])
            sp.wait_ge(xt_written, 32)
            sp.wait_ge(ones_ready, 1)
            load_x0(0)
            load_x(0, 0)
            write_tiles(0, range(1, TPB))
            sp.wait_ge(xt_written, 32 * TPB)
            fetch_indices(1)
            for t in range(TPB):
                step(t, t % 2, 1 if t == TPB - 1 else None)
            fetch_indices(2)
            with sp.Fori(1, NB - 2) as i:
                for k in range(TPB):
                    step(i * TPB + k, k % 2, i + 1 if k == TPB - 1 else None)
                fetch_indices(i + 2)
            for t in range(TPB * (NB - 2), NT - 1):
                step(t, t % 2, NB - 1 if t == TPB * (NB - 1) - 1 else None)
            last = Part(NT - 1)
            sp.wait_ge(z_ready, last.count(every, len(MODES[0]) + len(MODES[2])))
            for dst, src in ((WT1, wt1), (WT1C, wt1c), (WT2, wt2), (WT3[:], wt3), (BT1[:], bt1), (BT2[:], bt2),
                             (CT, ctxT)):
                sp.dma_start(dst, src).then_inc(wt_in, 16)
            step(NT - 1, 1, more=False)
            end = Part(NT)
            sp.wait_ge(z_ready, end.count(every, len(end.chunks)))
            load_sums(0)
            save_sums(1, NT - 1, 1)
            save_sums(2, NT - 1, 1)
            for k in range(3):
                sp.wait_ge(sums_out[k], 16 * NT)
            load_sums(1)
            sp.wait_ge(top_used, NH * TOP)
            sp.dma_start(out, Y).then_inc(y_out, 16)
            sp.wait_ge(y_out, 16)

        @block.scalar
        def _(act):
            def load(dst, src, s):
                act.dma_start(dst, src).then_inc(s, 16)

            load(W0A, w0a, w0_in)
            load(W0B, w0b, w0_in)
            load(WSA, ws[:, 0:half], ws_in)
            load(WSB, ws[:, half:NWB * O], ws_in)
            load(WF[:, NF0:NWF, :].rearrange("p c o -> p (c o)"), wf, wf_in)
            load(cb[:], cin_b, wf_in)
            flat = WH[:].rearrange("p c o -> p (c o)")
            act.wait_ge(ws_in, 32)
            nc.scalar.copy(flat[:, NS0 * O:NS0 * O + half], WSA).then_inc(wh_ready, 1)
            nc.scalar.copy(flat[:, NS0 * O + half:NWS * O], WSB).then_inc(wh_ready, 1)
            act.wait_ge(w0_folded, 1)
            nc.scalar.copy(flat[:, 0:NS0 * O], W0A[:, 0:NS0 * O]).then_inc(wh_ready, 1)
            act.wait_ge(wf_in, 32)

            def upper(part, r, like):
                k = part.chunks[r]
                if not split(k):
                    return
                act.wait_ge(z_ready, part.count(every, r) + 1)
                old = part.back(split, r, NZH)
                if old is not None:
                    act.wait_ge(used, part.count(every, old) + 1)
                n = len(k.blocks)
                nc.scalar.copy(ZH[:, part.buffer(split, r, NZH, like), 0:n, :],
                               Z[:, part.buffer(every, r, NZ, like), 0:n, :]).then_inc(zh_ready, 1)

            def spread(part, r, like, src, quads=True):
                k = part.chunks[r]
                pj = PJ[part.buffer(starts_spread, r, NPJ, like)]
                old = part.back(starts_spread, r, NPJ)
                if old is not None:
                    act.wait_ge(z_ready, part.count(every, old) + NG // WIDE)
                if k.layer == 0:
                    nc.scalar.copy(pj[:], src).then_inc(spread_ready, NQ)
                    return
                j = SPREADS.index(k.spread) - 1
                for q in range(NQ):
                    nc.scalar.copy(pj[Q * q:Q * q + Q, :], src[Q * j:Q * j + Q, :]).then_inc(spread_ready, 1)

            def bias0(t):
                act.wait_ge(raw[0], t + 1)
                nc.scalar.activation(acc[0][:], acc[0][:], ACT.Identity, bias=cb[:, 0:1]).then_inc(biased[0], 1)
                act.wait_ge(biased[0], t + 1)
                nc.scalar.activation(sq[0][:], acc[0][:], ACT.Square).then_inc(squared[0], 1)

            def bias1(t):
                act.wait_ge(raw[1], t + 1)
                nc.scalar.activation(PB[:], acc[1][:], ACT.Identity, bias=cb[:, 1:2]).then_inc(biased[1], 1)
                act.wait_ge(biased[1], t + 1)

            def square1(t):
                nc.scalar.activation(sq[1][:], PB[:], ACT.Square).then_inc(squared[1], 1)

            def bias2(t):
                act.wait_ge(scaled2, t + 1)
                nc.scalar.activation(acc[2][:], acc[2][:], ACT.Identity, bias=cb[:, 2:3]).then_inc(biased[2], 1)
                act.wait_ge(biased[2], t + 1)
                nc.scalar.activation(sq[2][:], acc[2][:], ACT.Square).then_inc(squared[2], 1)

            def take_root(k, t):
                act.wait_ge(norm2[k], t + 1)
                nc.scalar.activation(root[:, k, :], nrm[k], ACT.Sqrt).then_inc(rooted[k], 1)

            def top_blocks(which):
                for n in which:
                    h, o = divmod(n, TOP)
                    act.wait_ge(top_ready, n + 1)
                    if o < F1 // 128:
                        ins = nc.scalar.activation(H1[:, o, :], TB[n % 3][:], ACT.Relu, bias=BT1[:, o:o + 1])
                    elif o < TOP - 1:
                        o -= F1 // 128
                        ins = nc.scalar.activation(H2[:, o, :], TB[n % 3][:], ACT.Relu, bias=BT2[:, o:o + 1])
                    else:
                        ins = nc.scalar.copy(Y[0:1, h * R:h * R + R], TB[n % 3][0:1, :])
                    ins.then_inc(top_used, 1)

            def layer0_factor(t, like):
                act.wait_ge(x0_loaded, 16 * 7 * (t + 1))
                spread(Part(t), 0, like, X0[:, T_PART, :])

            def step(t, like, more=True):
                part = Part(t)
                n0, n2 = len(MODES[0]), len(MODES[2])

                def l2(c):
                    return n0 + c if part.kind == "middle" else c

                def l1(c):
                    return n0 + c if part.kind == "first" else n0 + n2 + c

                def spread1(j):
                    spread(part, l1(1 + j * 3), like, PA[:])

                def spread2(j):
                    spread(part, l2(1 + j * 3), like, PB[:])

                if part.kind != "last":
                    for r in range(n0):
                        upper(part, r, like)
                if part.kind == "first":
                    bias0(t)
                    take_root(0, t)
                else:
                    bias1(t - 1)
                    spread2(0)
                    spread2(1)
                    for c in range(n2):
                        upper(part, l2(c), like)
                        if c == 1:
                            square1(t - 1)
                        if c == 2 and part.kind == "middle":
                            bias0(t)
                        if c == 3:
                            spread2(2)
                        if c == 6:
                            spread2(3)
                        if c == 8:
                            take_root(1, t - 1)
                            if part.kind == "middle":
                                take_root(0, t)
                        if part.kind == "middle":
                            if c == 10:
                                act.wait_ge(p0_ready, t + 1)
                                spread1(0)
                            if c == 12:
                                spread1(1)
                if part.kind == "last":
                    bias2(t - 1)
                    act.wait_ge(wt_in, 16 * 7)
                    top_blocks(range(TOP_SPLIT))
                    take_root(2, t - 1)
                    return
                if part.kind == "first":
                    act.wait_ge(p0_ready, t + 1)
                    spread1(0)
                    spread1(1)
                for c in range(len(MODES[1])):
                    upper(part, l1(c), like)
                    if c == 3:
                        spread1(2)
                    if c == 6:
                        spread1(3)
                    if c == 5 and part.kind == "middle":
                        bias2(t - 1)
                    if c == 9 and more:
                        layer0_factor(t + 1, like + 1)
                    if c == 11 and part.kind == "middle":
                        take_root(2, t - 1)

            layer0_factor(0, 0)
            step(0, 0)
            with act.Fori(0, (NT - 2) // 2) as i:
                step(2 * i + 1, 1)
                step(2 * i + 2, 2)
            step(NT - 1, 1, more=False)
            step(NT, 2)

            top_blocks(range(TOP_SPLIT, NH * TOP))

        @block.vector
        def _(dve):
            nc.vector.memset(X0[Q * NF:128, T_B:T_A + 1, :], 0.0).then_inc(chain, 1)
            dve.wait_ge(chain, 1)
            nc.vector.memset(ones[:], 1.0).then_inc(ones_ready, 1)
            dve.wait_ge(w0_in, 32)
            nc.vector.tensor_tensor(W0A[:, 0:NS0 * O], W0A[:, 0:NS0 * O], W0B[:, 0:NS0 * O],
                                    ALU.add).then_inc(w0_folded, 1)
            nc.vector.tensor_tensor(WF[:, 0:NF0, :].rearrange("p c o -> p (c o)"), W0A[:, NS0 * O:C0 * O],
                                    W0B[:, NS0 * O:C0 * O], ALU.add)
            hi = WH[:].bitcast(fp32).rearrange("p c o -> p (c o)")
            lo = WL[:].rearrange("p c o -> p (c o)")
            cuts = [(NS0 * O, NS0 * O + half, WSA), (NS0 * O + half, NWS * O, WSB), (0, NS0 * O, W0A[:, 0:NS0 * O])]
            for n, (a, b, src) in enumerate(cuts):
                dve.wait_ge(wh_ready, n + 1)
                nc.vector.tensor_tensor(lo[:, a:b], src, hi[:, a:b], ALU.subtract).then_inc(w_ready, 1)
            dve.wait_ge(w_ready, 3)

            def form(part, r, like, par):
                k = part.chunks[r]
                old = part.back(every, r, NZ)
                if old is not None:
                    if by_pool(part.get(old)):
                        dve.wait_ge(zl_pool, part.count(by_pool, old) + 1)
                    elif by_vector(part.get(old)):
                        dve.wait_ge(zl_vector, part.count(by_vector, old) + 1)
                    else:
                        dve.wait_ge(used, part.count(every, old) + 1)
                n = len(k.blocks)
                pj = None
                if k.spread:
                    e = r if starts_spread(k) else part.back(starts_spread, r, 1)
                    pj = PJ[part.buffer(starts_spread, e, NPJ, like)]
                    if starts_spread(k):
                        dve.wait_ge(spread_ready, NQ * (part.count(starts_spread, r) + 1))
                    pj = pj[:, :].unsqueeze(1).to_broadcast([128, n, R])
                P = PA if k.layer == 1 else PB
                if k.layer == 0:
                    a = X[:, par, k.blocks[0]:k.blocks[0] + n, :] if pj is not None else X0[:, T_A:T_A + 1, :]
                    b = pj if pj is not None else X0[:, T_B:T_B + 1, :]
                elif pj is None:
                    a, b = X[:, par, S_FULL:NS, :], P[:, :].unsqueeze(1).to_broadcast([128, NF, R])
                else:
                    a, b = X[:, par, k.slots, :], pj
                nc.vector.tensor_tensor(Z[:, part.buffer(every, r, NZ, like), 0:n, :], a, b,
                                        ALU.mult).then_inc(z_ready, 1)

            def lower(part, r, like):
                k = part.get(r)
                if k is None or not by_vector(k):
                    return
                dve.wait_ge(zh_ready, part.count(split, r) + 1)
                old = part.back(split, r, NZL)
                if old is not None:
                    dve.wait_ge(used, part.count(every, old) + 1)
                n = len(k.blocks)
                nc.vector.tensor_tensor(ZL[:, part.buffer(split, r, NZL, like), 0:n, :],
                                        Z[:, part.buffer(every, r, NZ, like), 0:n, :],
                                        ZHf[:, part.buffer(split, r, NZH, like), 0:n, :],
                                        ALU.subtract).then_inc(zl_vector, 1)

            LINK = 4

            def reduce(k, t, src):
                dve.wait_ge(squared[k], t + 1)
                nc.vector.reduce_sum(sr[:, k, :], bd(src), axis=AX.X)
                nc.vector.reduce_sum(ss[:, k, :], bd(sq[k][:]), axis=AX.X).then_inc(summed[k], 1)

            def invert(k, t, n):
                def link(ins, m):
                    ins.then_inc(chain, 1)
                    dve.wait_ge(chain, n + m)

                dve.wait_ge(rooted[k], t + 1)
                link(nc.vector.reciprocal(rr[:, k, :], root[:, k, :]), 1)
                link(nc.vector.scalar_tensor_tensor(ra[:, k, :], rr[:, k, :], -0.5, nrm[k], ALU.mult, ALU.mult), 2)
                link(nc.vector.tensor_tensor(rb[:, k, :], ra[:, k, :], rr[:, k, :], ALU.mult), 3)
                link(nc.vector.scalar_tensor_tensor(inv[:, k, :], rb[:, k, :], 1.5, rr[:, k, :], ALU.add, ALU.mult), 4)

            def keep_sums(k, par, t=None):
                if t is not None:
                    dve.wait_ge(sums_out[k], 16 * (t - 1))
                nc.vector.tensor_tensor(sums[:, par, k, :], sr[:, k, :], inv[:, k, :],
                                        ALU.mult).then_inc(sums_ready[k], 1)

            def norm0(t, par, n):
                invert(0, t, n)
                keep_sums(0, par)
                nc.vector.tensor_tensor(bd(PA[:]), bd(acc[0][:]), bc_d(inv[:, 0, :]), ALU.mult).then_inc(p0_ready, 1)

            def scale2(t):
                dve.wait_ge(raw[2], t + 1)
                nc.vector.tensor_tensor(bd(acc[2][:]), bd(acc[2][:]), bc_d(inv[:, 1, :]), ALU.mult).then_inc(scaled2, 1)

            def step(t, like, par=None, loads=None):
                part = Part(t)
                n0, n2, n1 = map(len, (MODES[0], MODES[2], MODES[1]))
                n = 1 + LINK + 3 * LINK * (t - 1)
                r = 0

                flushed = 0

                def advance(par):
                    nonlocal r
                    form(part, r, like, par)
                    if r - LAG >= flushed:
                        lower(part, r - LAG, like)
                    r += 1

                def flush():
                    nonlocal flushed
                    for c in range(r - LAG, r):
                        lower(part, c, like)
                    flushed = r

                if part.kind == "middle":
                    flushed = -LAG
                if part.kind != "last":
                    dve.wait_ge(x_loaded[par], loads * (16 * 5))
                    for c in range(n0):
                        advance(par)
                if part.kind == "first":
                    flush()
                    reduce(0, t, acc[0][:])
                    norm0(t, par, 1)
                else:
                    if part.kind == "last":
                        flush()
                    dve.wait_ge(biased[1], t)
                    for c in range(n2):
                        advance(1 if par is None else 1 - par)
                        if c == 4:
                            reduce(1, t - 1, PB[:])
                            if part.kind == "middle":
                                reduce(0, t, acc[0][:])
                        if c == 9:
                            invert(1, t - 1, n)
                            keep_sums(1, *((1, t - 1) if par is None else (1 - par,)))
                            if part.kind == "middle":
                                norm0(t, par, n + LINK)
                if part.kind == "last":
                    flush()
                    scale2(t - 1)
                    reduce(2, t - 1, acc[2][:])
                    invert(2, t - 1, n + LINK)
                    keep_sums(2, 1, t - 1)
                    return
                dve.wait_ge(p0_ready, t + 1)
                for c in range(n1):
                    advance(par)
                    if part.kind == "middle":
                        if c == 4:
                            scale2(t - 1)
                        if c == 6:
                            reduce(2, t - 1, acc[2][:])
                        if c == 12:
                            invert(2, t - 1, n + 2 * LINK)
                            keep_sums(2, 1 - par)

            step(0, 0, 0, 1)
            with dve.Fori(0, (NT - 2) // 2) as i:
                step(2 * i + 1, 1, 1, i + 1)
                step(2 * i + 2, 2, 0, i + 2)
            step(NT - 1, 1, 1, NT // 2)
            step(NT, 2)

        @block.tensor
        def _(pe):
            def products(part, r, like):
                k = part.chunks[r]
                a = acc[k.layer][:]
                n = len(k.blocks)

                def take(W, slot, z, first, last):
                    for j, b in enumerate(k.blocks):
                        ins = nc.tensor.matmul(a, W[:, slot[k.layer, b], :], z[:, j, :],
                                               start=first and j == 0, stop=last and j == n - 1)
                    return ins

                if not split(k):
                    pe.wait_ge(z_ready, part.count(every, r) + 1)
                    ins = take(WF, SLOT_F, Z[:, part.buffer(every, r, NZ, like)], k.first, k.last)
                else:
                    zh = ZH[:, part.buffer(split, r, NZH, like)]
                    pe.wait_ge(zh_ready, part.count(split, r) + 1)
                    take(WH, SLOT_S, zh, k.first, False)
                    take(WL, SLOT_S, zh, False, False)
                    if by_pool(k):
                        pe.wait_ge(zl_pool, part.count(by_pool, r) + 1)
                    else:
                        pe.wait_ge(zl_vector, part.count(by_vector, r) + 1)
                    ins = take(WH, SLOT_S, ZL[:, part.buffer(split, r, NZL, like)], False, k.last)
                ins.then_inc(used, 1)
                if k.last:
                    pe.wait_ge(used, part.count(every, r) + 1)
                    pe.sem_inc(raw[k.layer], 1)

            def norm(k, t):
                pe.wait_ge(summed[k], t + 1)
                nc.tensor.matmul(nrm[k], ones[:], ss[:, k, :], start=True, stop=True).then_inc(norm2[k], 1)

            def step(t, like):
                part = Part(t)
                n0 = len(MODES[0])
                for r, k in enumerate(part.chunks):
                    if part.kind == "middle" and r == 0:
                        pe.wait_ge(p0_ready, t)
                    products(part, r, like)
                    if k.layer == 2 and k.c == 4:
                        norm(1, t - 1)
                        if part.kind == "middle":
                            norm(0, t)
                    if k.layer == 1 and k.c == 7 and part.kind == "middle":
                        norm(2, t - 1)
                    if part.kind == "first" and r == n0 - 1:
                        norm(0, t)
                if part.kind == "last":
                    top_blocks(range(TOP_SPLIT))
                    norm(2, t - 1)

            def top_blocks(which):
                for n in which:
                    h, o = divmod(n, TOP)
                    if o == 0:
                        pe.wait_ge(s_in[h], 16)
                        if h == 0:
                            pe.wait_ge(wt_in, 16 * 7)
                    if o == F1 // 128 or o == TOP - 1:
                        pe.wait_ge(top_used, n)
                    elif n > 2:
                        pe.wait_ge(top_used, n - 2)
                    a = TB[n % 3]
                    if o < F1 // 128:
                        u, cols = slice(o * 128, o * 128 + 128), slice(h * R, h * R + R)
                        for k in range(3):
                            nc.tensor.matmul(a[:], WT1[:, k, u], S[:, k, cols], start=(k == 0), stop=False)
                        last = nc.tensor.matmul(a[:], WT1C[:, u], CT[:, cols], start=False, stop=True)
                    elif o < TOP - 1:
                        u = slice((o - F1 // 128) * 128, (o - F1 // 128) * 128 + 128)
                        for k in range(F1 // 128):
                            last = nc.tensor.matmul(a[:], WT2[:, k, u], H1[:, k, :],
                                                    start=(k == 0), stop=(k == F1 // 128 - 1))
                    else:
                        for k in range(F2 // 128):
                            last = nc.tensor.matmul(a[0:1, :], WT3[:, k:k + 1], H2[:, k, :],
                                                    start=(k == 0), stop=(k == F2 // 128 - 1))
                    last.then_inc(top_ready, 1)

            pe.wait_ge(ones_ready, 1)
            pe.wait_ge(wf_in, 32)
            pe.wait_ge(w_ready, 3)
            step(0, 0)
            with pe.Fori(0, (NT - 2) // 2) as i:
                step(2 * i + 1, 1)
                step(2 * i + 2, 2)
            step(NT - 1, 1)
            step(NT, 2)

            top_blocks(range(TOP_SPLIT, NH * TOP))


def layer0_rows():
    a = np.full((C0, 128), M * M)
    b = np.full((C0, 128), M * M)

    def put(block, p, m, h):
        a[block, p] = m * M + h
        if m != h:
            b[block, p] = h * M + m

    for m in range(NQ * NG):
        for h in range(min(m + 1, Q)):
            put(m // NQ, (m % NQ) * Q + h, m, h)
    for f in range(NF):
        for h in range(Q):
            put(NG, f * Q + h, NQ * NG + f, h)
    for k in range(HALF):
        for m in range(TAIL):
            put(NG, NF * Q + k * TAIL + m, Q + m, Q + (m + k) % TAIL)
    return a, b


def layer12_rows():
    r = np.empty((C12, 128), np.int64)
    p = np.arange(128)
    for g in range(NG):
        for j in range(NQ):
            r[NQ * g + j] = (NQ * g + p // Q) * O + Q * j + p % Q
    for f in range(NF):
        r[NQ * NG + f] = (NQ * NG + f) * O + p
    return r


def kernel(**inputs):
    import concourse.bacc as bacc
    from concourse.bass_utils import run_bass_kernel_spmd

    given = {k: np.asarray(v) for k, v in inputs.items()}

    def blocks(w, rows):
        return w[rows].transpose(1, 0, 2).reshape(128, -1)

    a0, b0 = layer0_rows()
    w0 = np.concatenate([given["L0_rec_w0"], np.zeros((1, O), given["L0_rec_w0"].dtype)])
    r12 = layer12_rows()
    wt1, wt2 = given["W_top1"], given["W_top2"]

    def part(slots, layers):
        rows = {1: given["L0_rec_w1"], 2: given["L0_rec_w2"]}
        return np.concatenate([blocks(rows[layer], r12[[b]]) for layer, b in slots if layer in layers], axis=1)

    order0 = [b for layer, b in [*SLOT_S, *SLOT_F] if layer == 0]
    arrays = {
        "ids": given["ids"],
        **{f"tbl_{f}": given[f"tbl_{f}"] for f in range(M)},
        "ctxT": given["dense_ctx"].T,
        "w0a": blocks(w0, a0[order0]), "w0b": blocks(w0, b0[order0]),
        "wf": part(SLOT_F, (1, 2)), "ws": part(SLOT_S, (1, 2)),
        "cin_b": np.stack([given[f"L0_rec_b{k}"] for k in range(3)], axis=1),
        "wt1": wt1[:3 * O].reshape(3, O, F1).transpose(1, 0, 2), "wt1c": wt1[3 * O:],
        "bt1": given["b_top1"].reshape(-1, 128).T,
        "wt2": wt2.reshape(F1 // 128, 128, F2).transpose(1, 0, 2),
        "bt2": given["b_top2"].reshape(-1, 128).T,
        "wt3": given["W_top3"].reshape(F2 // 128, 128).T,
    }
    arrays = {f"in_{k}": np.ascontiguousarray(v) for k, v in arrays.items()}
    nc = bacc.Bacc("TRN2", target_bir_lowering=False, num_devices=1)
    ap = {k[3:]: nc.dram_tensor(k, v.shape, mybir.dt.from_np(v.dtype), kind="ExternalInput").ap()
          for k, v in arrays.items()}
    out = nc.dram_tensor("out_y", (1, B), mybir.dt.float32, kind="ExternalOutput").ap()
    cin_tower(nc, ap["ids"], [ap[f"tbl_{f}"] for f in range(M)], ap["ctxT"], ap["w0a"], ap["w0b"], ap["wf"],
              ap["ws"], ap["cin_b"], ap["wt1"], ap["wt1c"], ap["bt1"], ap["wt2"], ap["bt2"], ap["wt3"], out)
    r = run_bass_kernel_spmd(nc, [arrays], core_ids=[0])
    return r.results[0]["out_y"].reshape(B, 1)
```

```python
import numpy as np
import concourse.bass as bass
from concourse import mybir
from contextlib import ExitStack

B = 1024
M = 39
D = 16
O = 128
Q = 32
NQ = 4
R = 512
BT = R // D
NT = B // BT
NG = 9
NF = M - NQ * NG
C12 = NQ * NG + NF
C0 = NG + 1
TAIL = M - Q
HALF = TAIL // 2 + 1
XR = M + HALF - 1
BLK = 128
NB = B // BLK
TPB = BLK // BT
CTX = 16
CTX_ROWS = 3 * Q
F1, F2 = 512, 256
NH = B // R

S_FULL = NG
NS = S_FULL + NF
T_PART, T_B, T_A = range(3)
NT0 = 3

WIDE = 3
EARLY = 2 * WIDE
NZ = 5
NZH = 3
NZL = 3
NPJ = 3

MODES = {0: "FVGF", 1: "FGFGFGVGFGFVG", 2: "FGFGFGVGFGFGV"}
SPREADS = "sabcd"


class Chunk:

    def __init__(self, layer, c):
        self.layer, self.c, self.mode = layer, c, MODES[layer][c]
        if layer == 0:
            self.blocks = list(range(WIDE * c, min(WIDE * c + WIDE, C0)))
            self.spread = "s" if c < NG // WIDE else None
        elif c == 0:
            self.blocks = [NQ * NG + f for f in range(NF)]
            self.spread = None
        else:
            j, g = divmod(c - 1, NG // WIDE)
            self.blocks = [NQ * (g * WIDE + k) + j for k in range(WIDE)]
            self.slots = slice(g * WIDE, g * WIDE + WIDE)
            self.spread = SPREADS[1 + j]
        self.first, self.last = c == 0, c == len(MODES[layer]) - 1


def layer_chunks(layer):
    return [Chunk(layer, c) for c in range(len(MODES[layer]))]


class Part:

    def __init__(self, t):
        self.t = t
        static = isinstance(t, int)
        self.kind = "first" if static and t == 0 else "last" if static and t == NT else "middle"
        layers = {"first": [0, 1], "middle": [0, 2, 1], "last": [2]}[self.kind]
        self.chunks = [k for layer in layers for k in layer_chunks(layer)]
        self.before = [] if self.kind == "first" else layer_chunks(1)

    def count(self, what, r=0, at=None):
        t = self.t if at is None else at
        inside = self.before + self.chunks
        n = len(self.before)
        rel = sum(map(what, inside[n:n + r])) if r >= 0 else -sum(map(what, inside[n + r:n]))
        if self.kind == "first":
            return rel
        head = sum(map(what, layer_chunks(0) + layer_chunks(1)))
        every = head + sum(map(what, layer_chunks(2)))
        return t * every + (head - every + rel)

    def buffer(self, what, r, ring, like):
        return self.count(what, r, at=like) % ring

    def back(self, what, r, n):
        inside = self.before + self.chunks
        found = [k for k in range(len(self.before) + r) if what(inside[k])]
        if len(found) < n:
            assert self.kind == "first"
            return None
        return found[-n] - len(self.before)

    def get(self, r):
        inside = self.before + self.chunks
        k = r + len(self.before)
        return inside[k] if k >= 0 else None


def every(k):
    return 1


def split(k):
    return int(k.mode in "VG")


def by_vector(k):
    return int(k.mode == "V")


def by_pool(k):
    return int(k.mode == "G")


def starts_spread(k):
    c = k.c if k.layer == 0 else k.c - 1
    return int(k.spread is not None and c % (NG // WIDE) == 0)


_two = 2 * [k for layer in range(3) for k in layer_chunks(layer)]
for _what, _ring in ((every, NZ), (split, NZH), (split, NZL), (starts_spread, NPJ)):
    assert sum(map(_what, _two)) % _ring == 0


def layer_end(layer, t):
    n0, n1, n2 = (len(MODES[k]) for k in range(3))
    if layer == 2:
        part = Part(t + 1)
        return part.count(every, n2 if part.kind == "last" else n0 + n2)
    part = Part(t)
    return part.count(every, n0 if layer == 0 else len(part.chunks))


SLOT_F, SLOT_S = {}, {}
for _layer in range(3):
    for _k in layer_chunks(_layer):
        for _b in _k.blocks:
            _s = SLOT_S if split(_k) else SLOT_F
            _s[_layer, _b] = len(_s)
NWF, NWS = len(SLOT_F), len(SLOT_S)
NF0, NS0 = (sum(k[0] == 0 for k in s) for s in (SLOT_F, SLOT_S))
OLDEST_H, OLDEST_L = (Part(NT).count(split, len(MODES[2]), at=2) % ring for ring in (NZH, NZL))

REDUCE_AT, NORMS_AT, ROOTS_AT, INVERT_AT, SQUARE1_AT, BIAS0_AT = 4, 4, 8, 9, 1, 2
SCALE2_AT, BIAS2_AT, REDUCE2_AT = 5, 5, 7
SPREAD_AT = (3, 6, 10, 12)
SPREAD1_AT = (2, 6, 9)
LAG = 2
TOP_AT = 9
TOP_SPLIT = 2
TOP = F1 // 128 + F2 // 128 + 1


def cin_tower(nc, ids, tables, ctxT, w0a, w0b, wf, ws, cin_b, wt1, wt1c, bt1, wt2, bt2, wt3, out):
    fp32, fp32r, i32 = mybir.dt.float32, mybir.dt.float32r, mybir.dt.int32
    ALU, ACT, AX = mybir.AluOpType, mybir.ActivationFunctionType, mybir.AxisListType
    with ExitStack() as ctx:
        def sb(name, shape, dt=fp32):
            return ctx.enter_context(nc.sbuf_tensor(name, shape, dt))

        def sem(name):
            return ctx.enter_context(nc.semaphore(name))

        xt = nc.dram_tensor("xt_scratch", (NT, XR, R), fp32, kind="Internal").ap()
        S_all = nc.dram_tensor("sums_scratch", (3, O, B), fp32, kind="Internal").ap()

        idx = sb("idx", [BLK, M], i32)
        emb = sb("emb", [BLK, M * D])
        X = sb("X", [128, 2, NS, R])
        X0 = sb("X0", [128, NT0, R])
        Z = sb("Z", [128, NZ, WIDE, R])
        ZH = sb("ZH", [128, NZH, WIDE, R], fp32r)
        ZL = sb("ZL", [128, NZL, WIDE, R], fp32r)
        PA = sb("PA", [128, R])
        PB = sb("PB", [128, R])
        WF = sb("WF", [128, NWF, O])
        WH = sb("WH", [128, NWS, O], fp32r)
        WL = sb("WL", [128, NWS, O], fp32r)
        cb = sb("cb", [128, 3])
        ones = sb("ones", [128, 128])
        CTXW = sb("CTXW", [CTX_ROWS, F1], fp32r)
        WT3 = sb("WT3", [128, F2 // 128])
        BT1 = sb("BT1", [128, F1 // 128])
        BT2 = sb("BT2", [128, F2 // 128])
        sums = sb("sums", [128, 2, 3, BT])
        ss = sb("ss", [128, 3, BT])
        sr = sb("sr", [128, 3, BT])
        root = sb("root", [128, 3, BT])
        rr = sb("rr", [128, 3, BT])
        ra = sb("ra", [128, 3, BT])
        rb = sb("rb", [128, 3, BT])
        inv = sb("inv", [128, 3, BT])
        ZHf, ZLf = ZH[:].bitcast(fp32), ZL[:].bitcast(fp32)

        def cuts_of(a, rows, widths):
            at = [int(n) for n in np.cumsum([0, *widths])]
            return [a[0:rows[k], at[k]:at[k + 1]] for k in range(len(widths))]

        Xtop = X[:, 0, :, :].rearrange("p s r -> p (s r)")
        rows, widths = (128, 128, CTX_ROWS, CTX_ROWS), (3 * F1, F1 // 128 * F2, B, F1)
        WT1, WT2, CTXV_IN, CTXW_IN = cuts_of(Xtop, rows, widths)
        WT1H, WT2H, CTXV = cuts_of(WH[:].rearrange("p c o -> p (c o)"), rows, widths[:3])
        WT1L, WT2L = cuts_of(WL[:].rearrange("p c o -> p (c o)"), rows, widths[:2])
        WT1Hf, WT2Hf, CTXVf = cuts_of(WH[:].bitcast(fp32).rearrange("p c o -> p (c o)"), rows, widths[:3])
        assert sum(widths[:3]) <= sum(k[0] < 2 for k in SLOT_S) * O
        S = X[:, 1, 0:3 * B // R, :].rearrange("p s r -> p (s r)").rearrange("p (k b) -> p k b", k=3)
        SHf, SH, SL = ZHf[:, OLDEST_H], ZH[:, OLDEST_H], ZL[:, OLDEST_L]
        assert WIDE == 3 and F1 // 128 <= 2 * (WIDE - 1)

        def h1_part(a, oldest, ring, k):
            return a[:, (oldest + 1 + k // 2) % ring, k % 2, :]
        Zall = Z[:].rearrange("p a b c -> p (a b c)")
        H2 = Zall[:, 0:F2 // 128 * R].rearrange("p (k n) -> p k n", n=R)
        Y = Zall[0:1, F2 // 128 * R:F2 // 128 * R + B]
        at = F2 // 128 * R + B
        H1 = Zall[:, at:at + F1 // 128 * R].rearrange("p (k n) -> p k n", n=R)

        Xodd = X[:, 1, :, :].rearrange("p s r -> p (s r)")
        W0A, W0B = Xodd[:, 0:C0 * O], Xodd[:, C0 * O:2 * C0 * O]
        NWB = NWS - NS0
        half = NWB // 2 * O
        WSA, WSB = Zall[:, 0:half], Xodd[:, 2 * C0 * O:2 * C0 * O + NWB * O - half]

        def bank(name):
            return ctx.enter_context(nc.psum_tensor(name, [128, R], fp32))

        acc = [bank(f"acc{k}") for k in range(3)]
        sq = [bank("sq0"), bank("sq12")]
        sq.append(sq[1])
        PJ = [bank(f"PJ{k}") for k in range(NPJ)]
        TB = [acc[0], acc[1], PJ[0]]
        nrm = sq[0][:, 0:3 * BT].rearrange("p (k b) -> p k b", k=3)

        idx_in = sem("idx_in")
        gathered = sem("gathered")
        xt_written = sem("xt_written")
        steps_seen = sem("steps_seen")
        x_loaded = [sem("x_loaded_even"), sem("x_loaded_odd")]
        x0_loaded = sem("x0_loaded")
        early_gathered = sem("early_gathered")
        early_written = sem("early_written")
        early_loaded = sem("early_loaded")
        w0_in, ws_in, wf_in, wt_in = sem("w0_in"), sem("ws_in"), sem("wf_in"), sem("wt_in")
        w0_folded = sem("w0_folded")
        wh_ready = sem("wh_ready")
        w_ready = sem("w_ready")
        ones_ready = sem("ones_ready")
        spread_ready = sem("spread_ready")
        z_ready = sem("z_ready")
        zh_ready = sem("zh_ready")
        zl_vector = sem("zl_vector")
        zl_pool = sem("zl_pool")
        used = sem("used")
        biased = [sem(f"biased{k}") for k in range(3)]
        scaled2 = sem("scaled2")
        squared = [sem(f"squared{k}") for k in range(3)]
        summed = sem("summed")
        norm2 = sem("norm2")
        rooted = sem("rooted")
        p0_ready = sem("p0_ready")
        sums_ready = sem("sums_ready")
        sums_out = sem("sums_out")
        s_in = [sem(f"s_in{h}") for h in range(NH)]
        chain = sem("chain")
        top_high = sem("top_high")
        top_low_pool = sem("top_low_pool")
        top_low_vector = sem("top_low_vector")
        s_high, s_low = sem("s_high"), sem("s_low")
        h1_high, h1_low = sem("h1_high"), sem("h1_low")
        top_ready = sem("top_ready")
        top_used = sem("top_used")
        y_out = sem("y_out")

        block = ctx.enter_context(nc.Block())

        def bc_d(a):
            return a.unsqueeze(2).to_broadcast([128, BT, D])

        def bd(a):
            return a.rearrange("p (b d) -> p b d", d=D)

        @block.gpsimd
        def _(pool):
            def gather(fields, arrived=gathered):
                for f in fields:
                    nc.gpsimd.indirect_dma_start(
                        out=emb[:, f * D:(f + 1) * D], out_offset=None, in_=tables[f],
                        in_offset=bass.IndirectOffsetOnAxis(ap=idx[:, f:f + 1], axis=0),
                    ).then_inc(arrived, 16)

            def step(t, like, fields=range(0)):
                part = Part(t)
                mine = [r for r, k in enumerate(part.chunks) if by_pool(k)]
                for i, r in enumerate(mine):
                    k = part.chunks[r]
                    pool.wait_ge(zh_ready, part.count(split, r) + 1)
                    old = part.back(split, r, NZL)
                    if old is not None:
                        pool.wait_ge(used, part.count(every, old) + 1)
                    n = len(k.blocks)
                    z = Z[:, part.buffer(every, r, NZ, like), 0:n, :]
                    zh = ZHf[:, part.buffer(split, r, NZH, like), 0:n, :]
                    zl = ZL[:, part.buffer(split, r, NZL, like), 0:n, :]
                    nc.gpsimd.tensor_tensor(zl, z, zh, ALU.subtract).then_inc(zl_pool, 1)
                    gather(fields[len(fields) * i // len(mine):len(fields) * (i + 1) // len(mine)])

            def four(t):
                n = (t // TPB if isinstance(t, int) else t[0]) + 1
                at = t if isinstance(t, int) else t[0] * TPB
                pool.wait_ge(idx_in, 16 * n + 16)
                pool.sem_inc(steps_seen, 1)
                pool.wait_ge(xt_written, 32 * TPB * n)
                pool.sem_inc(steps_seen, 1)
                for k in range(3):
                    like = 0 if isinstance(t, int) and k == 0 else 1 + (k + 1) % 2
                    step(at + k, like, range(M * k // 3, M * (k + 1) // 3))
                step(at + 3, 1)

            pool.wait_ge(idx_in, 16)
            gather(range(Q), early_gathered)
            gather(range(Q, M))
            four(0)
            with pool.Fori(1, NB - 1) as i:
                four((i,))
            for t in range(TPB * (NB - 1), NT + 1):
                step(t, 1 + (t + 1) % 2)
            pool.wait_ge(top_high, 4)
            nc.gpsimd.tensor_tensor(WT2L, WT2, WT2Hf, ALU.subtract).then_inc(top_low_pool, 1)

        @block.sync
        def _(sp):
            def source(t, row, ap):
                return bass.AP(xt.tensor, t * (XR * R) + row * R, ap)

            def load_slots(t, par, a, b, arrived):
                for q in range(NQ):
                    sp.dma_start(X[Q * q:Q * q + Q, par, a:b, :],
                                 source(t, NQ * a + q, [[0, Q], [NQ * R, b - a], [1, R]])).then_inc(arrived, 16)

            def load_x(t, par):
                first = EARLY if isinstance(t, int) and t == 0 else 0
                load_slots(t, par, first, NG, x_loaded[par])
                sp.dma_start(X[:, par, S_FULL:NS, :],
                             source(t, NQ * NG, [[0, 128], [1, NF * R]])).then_inc(x_loaded[par], 16)

            def load_x0(t):
                load_x0_fields(t, x0_loaded)
                load_x0_pairs(t)

            def load_x0_fields(t, arrived):
                for q in range(NQ):
                    slots = slice(T_PART, T_B + 1) if q < NF else slice(T_PART, T_PART + 1)
                    ap = [[R, Q], [0, 2], [1, R]] if q < NF else [[R, Q], [1, R]]
                    sp.dma_start(X0[Q * q:Q * q + Q, slots, :], source(t, 0, ap)).then_inc(arrived, 16)

            def load_x0_pairs(t):
                rest = slice(Q * NF, Q * NF + HALF * TAIL)
                for dst, src in ((X0[0:Q * NF, T_A, :], source(t, NQ * NG, [[R, NF], [0, Q], [1, R]])),
                                 (X0[rest, T_A, :], source(t, Q, [[0, HALF], [R, TAIL], [1, R]])),
                                 (X0[rest, T_B, :], source(t, Q, [[R, HALF], [R, TAIL], [1, R]]))):
                    sp.dma_start(dst, src).then_inc(x0_loaded, 16)

            def fetch_indices(n):
                sp.dma_start(idx[:], ids[bass.ds(n * BLK, BLK), :]).then_inc(idx_in, 16)

            def write_tiles(n, ks, m0=0):
                for k in ks:
                    at = (n * TPB + k) * (XR * R)
                    e = emb[k * BT:(k + 1) * BT, :].rearrange("b (m d) -> b m d", d=D)
                    sp.dma_start(bass.AP(xt.tensor, at + m0 * R, [[D, BT], [R, M - m0], [1, D]]),
                                 e[:, m0:M, :]).then_inc(xt_written, 16)
                    sp.dma_start(bass.AP(xt.tensor, at + M * R, [[D, BT], [R, XR - M], [1, D]]),
                                 e[:, Q:Q + XR - M, :]).then_inc(xt_written, 16)

            def save_sums(t, par, ks=range(3)):
                sp.wait_ge(sums_ready, t + 1)
                k0 = ks[0]
                dst = bass.AP(S_all.tensor, t * BT + k0 * (O * B - BT), [[B, O], [O * B - BT, len(ks)], [1, BT]])
                sp.dma_start(dst, sums[:, par, k0:k0 + len(ks), :]).then_inc(sums_out, 16)

            def load_sums(h):
                sp.dma_start(S[:, :, h * R:h * R + R],
                             S_all[:, :, h * R:h * R + R].rearrange("k p b -> p k b")).then_inc(s_in[h], 16)

            def step(t, par, block=None, more=True):
                part = Part(t)
                n0 = len(MODES[0])
                if not isinstance(t, int) or t > 0:
                    sp.wait_ge(sums_out, 16 * t)
                if block is not None:
                    sp.wait_ge(gathered, 16 * M * block + 16 * (M - Q))
                    write_tiles(block, range(TPB))
                    sp.wait_ge(xt_written, 32 * TPB * block + 32 * TPB)
                if more:
                    sp.wait_ge(z_ready, part.count(every, n0))
                    load_x0(t + 1)
                if part.kind == "first":
                    sp.wait_ge(w_ready, 3)
                    load_x(1, 1)
                elif more:
                    sp.wait_ge(z_ready, part.count(every, n0 + len(MODES[2])))
                    load_x(t + 1, 1 - par)
                save_sums(t, par, range(min(t + 1, 3) if isinstance(t, int) else 3))

            fetch_indices(0)
            sp.wait_ge(early_gathered, 16 * Q)
            sp.dma_start(bass.AP(xt.tensor, 0, [[D, BT], [R, Q], [1, D]]),
                         emb[0:BT, 0:Q * D].rearrange("b (m d) -> b m d", d=D)).then_inc(early_written, 16)
            sp.wait_ge(early_written, 16)
            sp.wait_ge(ones_ready, 1)
            load_x0_fields(0, early_loaded)
            load_slots(0, 0, 0, EARLY, early_loaded)
            sp.wait_ge(gathered, 16 * (M - Q))
            write_tiles(0, [0], Q)
            sp.wait_ge(xt_written, 32)
            load_x(0, 0)
            load_x0_pairs(0)
            write_tiles(0, range(1, TPB))
            sp.wait_ge(xt_written, 32 * TPB)
            fetch_indices(1)
            for t in range(TPB):
                step(t, t % 2, 1 if t == TPB - 1 else None)
            fetch_indices(2)
            with sp.Fori(1, NB - 2) as i:
                for k in range(TPB):
                    step(i * TPB + k, k % 2, i + 1 if k == TPB - 1 else None)
                fetch_indices(i + 2)
            for t in range(TPB * (NB - 2), NT - 1):
                step(t, t % 2, NB - 1 if t == TPB * (NB - 1) - 1 else None)
            last = Part(NT - 1)
            sp.wait_ge(z_ready, last.count(every, len(MODES[0]) + len(MODES[2])))
            wt = [wt1.rearrange("p k n -> p (k n)"), wt2.rearrange("p k n -> p (k n)")]
            for dst, src in ((CTXW_IN, wt1c), (CTXV_IN, ctxT), (WT1, wt[0]), (WT2, wt[1]), (WT3[:], wt3),
                             (BT1[:], bt1), (BT2[:], bt2)):
                sp.dma_start(dst, src).then_inc(wt_in, 16)
            step(NT - 1, 1, more=False)
            end = Part(NT)
            sp.wait_ge(z_ready, end.count(every, len(end.chunks)))
            load_sums(0)
            save_sums(NT, 0, range(1, 3))
            save_sums(NT + 1, 1, range(2, 3))
            sp.wait_ge(sums_out, 16 * (NT + 2))
            load_sums(1)
            sp.wait_ge(top_used, NH * TOP)
            sp.dma_start(out, Y).then_inc(y_out, 16)
            sp.wait_ge(y_out, 16)

        @block.scalar
        def _(act):
            def load(dst, src, s):
                act.dma_start(dst, src).then_inc(s, 16)

            load(W0A, w0a, w0_in)
            load(W0B, w0b, w0_in)
            load(WSA, ws[:, 0:half], ws_in)
            load(WSB, ws[:, half:NWB * O], ws_in)
            load(WF[:, NF0:NWF, :].rearrange("p c o -> p (c o)"), wf, wf_in)
            load(cb[:], cin_b, wf_in)
            flat = WH[:].rearrange("p c o -> p (c o)")
            act.wait_ge(ws_in, 32)
            nc.scalar.copy(flat[:, NS0 * O:NS0 * O + half], WSA).then_inc(wh_ready, 1)
            nc.scalar.copy(flat[:, NS0 * O + half:NWS * O], WSB).then_inc(wh_ready, 1)
            act.wait_ge(w0_folded, 1)
            nc.scalar.copy(flat[:, 0:NS0 * O], W0A[:, 0:NS0 * O]).then_inc(wh_ready, 1)
            act.wait_ge(wf_in, 32)

            def upper(part, r, like):
                k = part.chunks[r]
                if not split(k):
                    return
                act.wait_ge(z_ready, part.count(every, r) + 1)
                old = part.back(split, r, NZH)
                if old is not None:
                    act.wait_ge(used, part.count(every, old) + 1)
                n = len(k.blocks)
                nc.scalar.copy(ZH[:, part.buffer(split, r, NZH, like), 0:n, :],
                               Z[:, part.buffer(every, r, NZ, like), 0:n, :]).then_inc(zh_ready, 1)

            def spread(part, r, like, src):
                k = part.chunks[r]
                pj = PJ[part.buffer(starts_spread, r, NPJ, like)]
                old = part.back(starts_spread, r, NPJ)
                if old is not None:
                    act.wait_ge(z_ready, part.count(every, old) + NG // WIDE)
                if k.layer == 0:
                    nc.scalar.copy(pj[:], src).then_inc(spread_ready, NQ)
                    return
                j = SPREADS.index(k.spread) - 1
                for q in range(NQ):
                    nc.scalar.copy(pj[Q * q:Q * q + Q, :], src[Q * j:Q * j + Q, :]).then_inc(spread_ready, 1)

            def bias0(t):
                act.wait_ge(used, layer_end(0, t))
                nc.scalar.activation(acc[0][:], acc[0][:], ACT.Identity, bias=cb[:, 0:1]).then_inc(biased[0], 1)
                act.wait_ge(biased[0], t + 1)
                nc.scalar.activation(sq[0][:], acc[0][:], ACT.Square).then_inc(squared[0], 1)

            def bias1(t):
                act.wait_ge(used, layer_end(1, t))
                nc.scalar.activation(PB[:], acc[1][:], ACT.Identity, bias=cb[:, 1:2]).then_inc(biased[1], 1)
                act.wait_ge(biased[1], t + 1)

            def square1(t):
                nc.scalar.activation(sq[1][:], PB[:], ACT.Square).then_inc(squared[1], 1)

            def bias2(t):
                act.wait_ge(scaled2, t + 1)
                nc.scalar.activation(acc[2][:], acc[2][:], ACT.Identity, bias=cb[:, 2:3]).then_inc(biased[2], 1)
                act.wait_ge(biased[2], t + 1)
                nc.scalar.activation(sq[2][:], acc[2][:], ACT.Square).then_inc(squared[2], 1)

            def take_roots(t):
                act.wait_ge(norm2, t + 1)
                nc.scalar.activation(root[:], nrm, ACT.Sqrt).then_inc(rooted, 1)

            def top_uppers():
                act.wait_ge(wt_in, 16 * 7)
                for high, whole in ((CTXW[:], CTXW_IN), (CTXV, CTXV_IN), (WT1H, WT1), (WT2H, WT2)):
                    nc.scalar.copy(high, whole).then_inc(top_high, 1)

            def sums_upper(h):
                act.wait_ge(s_in[h], 16)
                if h == 0:
                    end = Part(NT)
                    act.wait_ge(used, end.count(every, end.back(split, len(end.chunks), NZH)) + 1)
                else:
                    act.wait_ge(top_ready, (h - 1) * TOP + F1 // 128)
                nc.scalar.copy(SH, S[:, :, h * R:h * R + R]).then_inc(s_high, 1)

            def top_blocks(which):
                for n in which:
                    h, o = divmod(n, TOP)
                    act.wait_ge(top_ready, n + 1)
                    if o < F1 // 128:
                        nc.scalar.activation(H1[:, o, :], TB[n % 3][:], ACT.Relu,
                                             bias=BT1[:, o:o + 1]).then_inc(top_used, 1)
                        act.wait_ge(top_used, n + 1)
                        nc.scalar.copy(h1_part(ZH, OLDEST_H, NZH, o), H1[:, o, :]).then_inc(h1_high, 1)
                        continue
                    if o < TOP - 1:
                        o -= F1 // 128
                        ins = nc.scalar.activation(H2[:, o, :], TB[n % 3][:], ACT.Relu, bias=BT2[:, o:o + 1])
                    else:
                        ins = nc.scalar.copy(Y[0:1, h * R:h * R + R], TB[n % 3][0:1, :])
                    ins.then_inc(top_used, 1)
                    if h < NH - 1 and o == 0:
                        sums_upper(h + 1)

            def layer0_factor(t, like):
                if isinstance(t, int) and t == 0:
                    act.wait_ge(early_loaded, 16 * 2 * NQ)
                else:
                    act.wait_ge(x0_loaded, 16 * 7 * t + 16 * 3)
                spread(Part(t), 0, like, X0[:, T_PART, :])

            def step(t, like, more=True):
                part = Part(t)
                n0, n2 = len(MODES[0]), len(MODES[2])

                def l2(c):
                    return n0 + c if part.kind == "middle" else c

                def l1(c):
                    return n0 + c if part.kind == "first" else n0 + n2 + c

                def spread1(j):
                    spread(part, l1(1 + j * 3), like, PA[:])

                def spread2(j):
                    spread(part, l2(1 + j * 3), like, PB[:])

                if part.kind != "last":
                    for r in range(n0):
                        upper(part, r, like)
                if part.kind == "first":
                    bias0(t)
                    take_roots(t)
                else:
                    bias1(t - 1)
                    spread2(0)
                    spread2(1)
                    for c in range(n2):
                        upper(part, l2(c), like)
                        if c == SQUARE1_AT:
                            square1(t - 1)
                        if c == BIAS0_AT and part.kind == "middle":
                            bias0(t)
                        if c == SPREAD_AT[0]:
                            spread2(2)
                        if c == SPREAD_AT[1]:
                            spread2(3)
                        if c == ROOTS_AT:
                            take_roots(t)
                        if c == TOP_AT and part.kind == "last":
                            top_uppers()
                        if part.kind == "middle":
                            if c == SPREAD_AT[2]:
                                act.wait_ge(p0_ready, t + 1)
                                spread1(0)
                            if c == SPREAD_AT[3]:
                                spread1(1)
                if part.kind == "last":
                    sums_upper(0)
                    bias2(t - 1)
                    top_blocks(range(TOP_SPLIT))
                    take_roots(t + 1)
                    return
                if part.kind == "first":
                    act.wait_ge(p0_ready, t + 1)
                    spread1(0)
                    spread1(1)
                for c in range(len(MODES[1])):
                    upper(part, l1(c), like)
                    if c == SPREAD1_AT[0]:
                        spread1(2)
                    if c == SPREAD1_AT[1]:
                        spread1(3)
                    if c == BIAS2_AT and part.kind == "middle":
                        bias2(t - 1)
                    if c == SPREAD1_AT[2] and more:
                        layer0_factor(t + 1, like + 1)

            layer0_factor(0, 0)
            step(0, 0)
            with act.Fori(0, (NT - 2) // 2) as i:
                step(2 * i + 1, 1)
                step(2 * i + 2, 2)
            step(NT - 1, 1, more=False)
            step(NT, 2)

            top_blocks(range(TOP_SPLIT, NH * TOP))

        @block.vector
        def _(dve):
            nc.vector.memset(X0[Q * NF:128, T_B:T_A + 1, :], 0.0).then_inc(chain, 1)
            nc.vector.memset(ss[:], 1.0).then_inc(chain, 1)
            nc.vector.memset(sr[:], 0.0).then_inc(chain, 1)
            dve.wait_ge(chain, 3)
            nc.vector.memset(ones[:], 1.0).then_inc(ones_ready, 1)
            dve.wait_ge(w0_in, 32)
            nc.vector.tensor_tensor(W0A[:, 0:NS0 * O], W0A[:, 0:NS0 * O], W0B[:, 0:NS0 * O],
                                    ALU.add).then_inc(w0_folded, 1)
            nc.vector.tensor_tensor(WF[:, 0:NF0, :].rearrange("p c o -> p (c o)"), W0A[:, NS0 * O:C0 * O],
                                    W0B[:, NS0 * O:C0 * O], ALU.add)
            hi = WH[:].bitcast(fp32).rearrange("p c o -> p (c o)")
            lo = WL[:].rearrange("p c o -> p (c o)")
            cuts = [(NS0 * O, NS0 * O + half, WSA), (NS0 * O + half, NWS * O, WSB), (0, NS0 * O, W0A[:, 0:NS0 * O])]
            for n, (a, b, src) in enumerate(cuts):
                dve.wait_ge(wh_ready, n + 1)
                nc.vector.tensor_tensor(lo[:, a:b], src, hi[:, a:b], ALU.subtract).then_inc(w_ready, 1)
            dve.wait_ge(w_ready, 3)

            def form(part, r, like, par):
                k = part.chunks[r]
                old = part.back(every, r, NZ)
                if old is not None:
                    if by_pool(part.get(old)):
                        dve.wait_ge(zl_pool, part.count(by_pool, old) + 1)
                    elif by_vector(part.get(old)):
                        dve.wait_ge(zl_vector, part.count(by_vector, old) + 1)
                    else:
                        dve.wait_ge(used, part.count(every, old) + 1)
                n = len(k.blocks)
                pj = None
                if k.spread:
                    e = r if starts_spread(k) else part.back(starts_spread, r, 1)
                    pj = PJ[part.buffer(starts_spread, e, NPJ, like)]
                    if starts_spread(k):
                        dve.wait_ge(spread_ready, NQ * (part.count(starts_spread, r) + 1))
                    pj = pj[:, :].unsqueeze(1).to_broadcast([128, n, R])
                P = PA if k.layer == 1 else PB
                if k.layer == 0:
                    a = X[:, par, k.blocks[0]:k.blocks[0] + n, :] if pj is not None else X0[:, T_A:T_A + 1, :]
                    b = pj if pj is not None else X0[:, T_B:T_B + 1, :]
                elif pj is None:
                    a, b = X[:, par, S_FULL:NS, :], P[:, :].unsqueeze(1).to_broadcast([128, NF, R])
                else:
                    a, b = X[:, par, k.slots, :], pj
                nc.vector.tensor_tensor(Z[:, part.buffer(every, r, NZ, like), 0:n, :], a, b,
                                        ALU.mult).then_inc(z_ready, 1)

            def lower(part, r, like):
                k = part.get(r)
                if k is None or not by_vector(k):
                    return
                dve.wait_ge(zh_ready, part.count(split, r) + 1)
                old = part.back(split, r, NZL)
                if old is not None:
                    dve.wait_ge(used, part.count(every, old) + 1)
                n = len(k.blocks)
                nc.vector.tensor_tensor(ZL[:, part.buffer(split, r, NZL, like), 0:n, :],
                                        Z[:, part.buffer(every, r, NZ, like), 0:n, :],
                                        ZHf[:, part.buffer(split, r, NZH, like), 0:n, :],
                                        ALU.subtract).then_inc(zl_vector, 1)

            LINK = 4

            def reduce(k, t, src):
                dve.wait_ge(squared[k], t + 1)
                nc.vector.reduce_sum(sr[:, k, :], bd(src), axis=AX.X)
                return nc.vector.reduce_sum(ss[:, k, :], bd(sq[k][:]), axis=AX.X)

            def invert(t, par):
                def link(ins, m):
                    ins.then_inc(chain, 1)
                    dve.wait_ge(chain, LINK * t + (3 + m))

                dve.wait_ge(rooted, t + 1)
                link(nc.vector.reciprocal(rr[:], root[:]), 1)
                link(nc.vector.scalar_tensor_tensor(ra[:], rr[:], -0.5, nrm, ALU.mult, ALU.mult), 2)
                link(nc.vector.tensor_tensor(rb[:], ra[:], rr[:], ALU.mult), 3)
                link(nc.vector.scalar_tensor_tensor(inv[:], rb[:], 1.5, rr[:], ALU.add, ALU.mult), 4)
                if isinstance(t, int) and t >= NT:
                    dve.wait_ge(sums_out, 16 * (t - 1))
                nc.vector.tensor_tensor(sums[:, par, :, :], sr[:], inv[:], ALU.mult).then_inc(sums_ready, 1)

            def normalise0(t):
                nc.vector.tensor_tensor(bd(PA[:]), bd(acc[0][:]), bc_d(inv[:, 0, :]), ALU.mult).then_inc(p0_ready, 1)

            def scale2(t):
                dve.wait_ge(used, layer_end(2, t))
                nc.vector.tensor_tensor(bd(acc[2][:]), bd(acc[2][:]), bc_d(inv[:, 1, :]),
                                        ALU.mult).then_inc(scaled2, 1)

            def step(t, like, par=None, loads=None):
                part = Part(t)
                n0, n2, n1 = map(len, (MODES[0], MODES[2], MODES[1]))
                r = 0

                flushed = 0

                def advance(par):
                    nonlocal r
                    form(part, r, like, par)
                    if r - LAG >= flushed:
                        lower(part, r - LAG, like)
                    r += 1

                def flush():
                    nonlocal flushed
                    for c in range(r - LAG, r):
                        lower(part, c, like)
                    flushed = r

                if part.kind == "middle":
                    flushed = -LAG
                if part.kind != "last":
                    if part.kind == "first":
                        dve.wait_ge(early_loaded, 16 * 2 * NQ)
                        for c in range(EARLY // WIDE):
                            advance(par)
                        dve.wait_ge(x0_loaded, 16 * 3)
                    dve.wait_ge(x_loaded[par], loads * (16 * 5))
                    for c in range(r, n0):
                        advance(par)
                if part.kind == "first":
                    flush()
                    reduce(0, t, acc[0][:]).then_inc(summed, 1)
                    invert(t, par)
                    normalise0(t)
                else:
                    if part.kind == "last":
                        flush()
                    dve.wait_ge(biased[1], t)
                    for c in range(n2):
                        advance(1 if par is None else 1 - par)
                        if c == REDUCE_AT:
                            ins = reduce(1, t - 1, PB[:])
                            if part.kind == "middle":
                                ins = reduce(0, t, acc[0][:])
                            ins.then_inc(summed, 1)
                        if c == INVERT_AT:
                            invert(t, 0 if par is None else par)
                            if part.kind == "middle":
                                normalise0(t)
                if part.kind == "last":
                    flush()
                    dve.wait_ge(top_high, 4)
                    wl, cl = slice(Q, Q + CTX), slice(2 * Q, 2 * Q + CTX)
                    for low, whole, high in ((CTXW[wl, :], CTXW_IN[wl, :], CTXW[:].bitcast(fp32)[wl, :]),
                                             (CTXV[cl, :], CTXV_IN[cl, :], CTXVf[cl, :]),
                                             (WT1L, WT1, WT1Hf)):
                        nc.vector.tensor_tensor(low, whole, high, ALU.subtract).then_inc(top_low_vector, 1)
                    sums_lower(0)
                    scale2(t - 1)
                    reduce(2, t - 1, acc[2][:]).then_inc(summed, 1)
                    h1_lowers(range(TOP_SPLIT))
                    invert(t + 1, 1)
                    h1_lowers(range(TOP_SPLIT, F1 // 128))
                    for h in range(1, NH):
                        sums_lower(h)
                        h1_lowers(range(h * F1 // 128, (h + 1) * F1 // 128))
                    return
                dve.wait_ge(p0_ready, t + 1)
                for c in range(n1):
                    advance(par)
                    if part.kind == "middle":
                        if c == SCALE2_AT:
                            scale2(t - 1)
                        if c == REDUCE2_AT:
                            reduce(2, t - 1, acc[2][:])

            def sums_lower(h):
                dve.wait_ge(s_high, h + 1)
                if h == 0:
                    end = Part(NT)
                    dve.wait_ge(used, end.count(every, end.back(split, len(end.chunks), NZL)) + 1)
                nc.vector.tensor_tensor(SL, S[:, :, h * R:h * R + R], SHf, ALU.subtract).then_inc(s_low, 1)

            def h1_lowers(which):
                for m in which:
                    o = m % (F1 // 128)
                    dve.wait_ge(h1_high, m + 1)
                    nc.vector.tensor_tensor(h1_part(ZL, OLDEST_L, NZL, o), H1[:, o, :],
                                            h1_part(ZHf, OLDEST_H, NZH, o), ALU.subtract).then_inc(h1_low, 1)

            step(0, 0, 0, 1)
            with dve.Fori(0, (NT - 2) // 2) as i:
                step(2 * i + 1, 1, 1, i + 1)
                step(2 * i + 2, 2, 0, i + 2)
            step(NT - 1, 1, 1, NT // 2)
            step(NT, 2)

        @block.tensor
        def _(pe):
            def products(part, r, like):
                k = part.chunks[r]
                a = acc[k.layer][:]
                n = len(k.blocks)

                def take(W, slot, z, first, last):
                    for j, b in enumerate(k.blocks):
                        ins = nc.tensor.matmul(a, W[:, slot[k.layer, b], :], z[:, j, :],
                                               start=first and j == 0, stop=last and j == n - 1)
                    return ins

                if not split(k):
                    pe.wait_ge(z_ready, part.count(every, r) + 1)
                    ins = take(WF, SLOT_F, Z[:, part.buffer(every, r, NZ, like)], k.first, k.last)
                else:
                    zh = ZH[:, part.buffer(split, r, NZH, like)]
                    pe.wait_ge(zh_ready, part.count(split, r) + 1)
                    take(WH, SLOT_S, zh, k.first, False)
                    take(WL, SLOT_S, zh, False, False)
                    if by_pool(k):
                        pe.wait_ge(zl_pool, part.count(by_pool, r) + 1)
                    else:
                        pe.wait_ge(zl_vector, part.count(by_vector, r) + 1)
                    ins = take(WH, SLOT_S, ZL[:, part.buffer(split, r, NZL, like)], False, k.last)
                ins.then_inc(used, 1)

            def norms(t):
                pe.wait_ge(summed, t + 1)
                nc.tensor.matmul(nrm, ones[:], ss[:], start=True, stop=True).then_inc(norm2, 1)

            def step(t, like):
                part = Part(t)
                n0 = len(MODES[0])
                for r, k in enumerate(part.chunks):
                    if part.kind == "middle" and r == 0:
                        pe.wait_ge(p0_ready, t)
                    products(part, r, like)
                    if (k.layer == 2 and k.c == NORMS_AT) or (part.kind == "first" and r == n0 - 1):
                        norms(t)
                if part.kind == "last":
                    top_blocks(range(TOP_SPLIT))
                    norms(t + 1)

            def top_blocks(which):
                for n in which:
                    h, o = divmod(n, TOP)
                    if n > 2:
                        pe.wait_ge(top_used, n - 2)
                    a = TB[n % 3]
                    if o < F1 // 128:
                        def w1(W, k):
                            return W[:, k * F1 + o * 128:k * F1 + o * 128 + 128]

                        if n == 0:
                            pe.wait_ge(top_high, 4)
                        if o == 0:
                            pe.wait_ge(s_high, h + 1)
                        for k in range(3):
                            nc.tensor.matmul(a[:], w1(WT1H, k), SH[:, k, :], start=(k == 0), stop=False)
                        if n == 0:
                            pe.wait_ge(top_low_vector, 3)
                        nc.tensor.matmul(a[:], CTXW[:, o * 128:o * 128 + 128], CTXV[:, h * R:h * R + R],
                                         start=False, stop=False)
                        for k in range(3):
                            nc.tensor.matmul(a[:], w1(WT1L, k), SH[:, k, :], start=False, stop=False)
                        if o == 0:
                            pe.wait_ge(s_low, h + 1)
                        for k in range(3):
                            last = nc.tensor.matmul(a[:], w1(WT1H, k), SL[:, k, :], start=False, stop=(k == 2))
                    elif o < TOP - 1:
                        u = (o - F1 // 128) * 128
                        for k in range(F1 // 128):
                            m = h * F1 // 128 + k + 1
                            w = slice(k * F2 + u, k * F2 + u + 128)
                            high = h1_part(ZH, OLDEST_H, NZH, k)
                            if n == F1 // 128 and k == 0:
                                pe.wait_ge(top_low_pool, 1)
                            if o == F1 // 128:
                                pe.wait_ge(h1_high, m)
                            nc.tensor.matmul(a[:], WT2H[:, w], high, start=(k == 0), stop=False)
                            nc.tensor.matmul(a[:], WT2L[:, w], high, start=False, stop=False)
                            if o == F1 // 128:
                                pe.wait_ge(h1_low, m)
                            last = nc.tensor.matmul(a[:], WT2H[:, w], h1_part(ZL, OLDEST_L, NZL, k),
                                                    start=False, stop=(k == F1 // 128 - 1))
                    else:
                        for k in range(F2 // 128):
                            pe.wait_ge(top_used, n - F2 // 128 + k + 1)
                            last = nc.tensor.matmul(a[0:1, :], WT3[:, k:k + 1], H2[:, k, :],
                                                    start=(k == 0), stop=(k == F2 // 128 - 1))
                    last.then_inc(top_ready, 1)

            pe.wait_ge(ones_ready, 1)
            pe.wait_ge(wf_in, 32)
            pe.wait_ge(w_ready, 3)
            step(0, 0)
            with pe.Fori(0, (NT - 2) // 2) as i:
                step(2 * i + 1, 1)
                step(2 * i + 2, 2)
            step(NT - 1, 1)
            step(NT, 2)

            top_blocks(range(TOP_SPLIT, NH * TOP))


def layer0_rows():
    a = np.full((C0, 128), M * M)
    b = np.full((C0, 128), M * M)

    def put(block, p, m, h):
        a[block, p] = m * M + h
        if m != h:
            b[block, p] = h * M + m

    for m in range(NQ * NG):
        for h in range(min(m + 1, Q)):
            put(m // NQ, (m % NQ) * Q + h, m, h)
    for f in range(NF):
        for h in range(Q):
            put(NG, f * Q + h, NQ * NG + f, h)
    for k in range(HALF):
        for m in range(TAIL):
            put(NG, NF * Q + k * TAIL + m, Q + m, Q + (m + k) % TAIL)
    return a, b


def layer12_rows():
    r = np.empty((C12, 128), np.int64)
    p = np.arange(128)
    for g in range(NG):
        for j in range(NQ):
            r[NQ * g + j] = (NQ * g + p // Q) * O + Q * j + p % Q
    for f in range(NF):
        r[NQ * NG + f] = (NQ * NG + f) * O + p
    return r


def kernel(**inputs):
    import concourse.bacc as bacc
    from concourse.bass_utils import run_bass_kernel_spmd

    given = {k: np.asarray(v) for k, v in inputs.items()}

    def blocks(w, rows):
        return w[rows].transpose(1, 0, 2).reshape(128, -1)

    a0, b0 = layer0_rows()
    w0 = np.concatenate([given["L0_rec_w0"], np.zeros((1, O), given["L0_rec_w0"].dtype)])
    r12 = layer12_rows()
    wt1, wt2 = given["W_top1"], given["W_top2"]

    def part(slots, layers):
        rows = {1: given["L0_rec_w1"], 2: given["L0_rec_w2"]}
        return np.concatenate([blocks(rows[layer], r12[[b]]) for layer, b in slots if layer in layers], axis=1)

    def stack3(a):
        c = np.zeros((CTX_ROWS, a.shape[1]), a.dtype)
        for q in range(3):
            c[Q * q:Q * q + CTX] = a
        return c

    order0 = [b for layer, b in [*SLOT_S, *SLOT_F] if layer == 0]
    arrays = {
        "ids": given["ids"],
        **{f"tbl_{f}": given[f"tbl_{f}"] for f in range(M)},
        "ctxT": stack3(given["dense_ctx"].T),
        "w0a": blocks(w0, a0[order0]), "w0b": blocks(w0, b0[order0]),
        "wf": part(SLOT_F, (1, 2)), "ws": part(SLOT_S, (1, 2)),
        "cin_b": np.stack([given[f"L0_rec_b{k}"] for k in range(3)], axis=1),
        "wt1": wt1[:3 * O].reshape(3, O, F1).transpose(1, 0, 2), "wt1c": stack3(wt1[3 * O:]),
        "bt1": given["b_top1"].reshape(-1, 128).T,
        "wt2": wt2.reshape(F1 // 128, 128, F2).transpose(1, 0, 2),
        "bt2": given["b_top2"].reshape(-1, 128).T,
        "wt3": given["W_top3"].reshape(F2 // 128, 128).T,
    }
    arrays = {f"in_{k}": np.ascontiguousarray(v) for k, v in arrays.items()}
    nc = bacc.Bacc("TRN2", target_bir_lowering=False, num_devices=1)
    ap = {k[3:]: nc.dram_tensor(k, v.shape, mybir.dt.from_np(v.dtype), kind="ExternalInput").ap()
          for k, v in arrays.items()}
    out = nc.dram_tensor("out_y", (1, B), mybir.dt.float32, kind="ExternalOutput").ap()
    cin_tower(nc, ap["ids"], [ap[f"tbl_{f}"] for f in range(M)], ap["ctxT"], ap["w0a"], ap["w0b"], ap["wf"],
              ap["ws"], ap["cin_b"], ap["wt1"], ap["wt1c"], ap["bt1"], ap["wt2"], ap["bt2"], ap["wt3"], out)
    r = run_bass_kernel_spmd(nc, [arrays], core_ids=[0])
    return r.results[0]["out_y"].reshape(B, 1)
```
